# Optimizing a Trainium2 kernel written in Bass

```python
import numpy as np
import jax
import jax.numpy as jnp

def _softmax(x, axis=-1):
    return jax.nn.softmax(x, axis=axis)

def _gelu(x):
    return jax.nn.gelu(x, approximate=True)

def _silu(x):
    return jax.nn.silu(x)

def _sigmoid(x):
    return jax.nn.sigmoid(x)

def _layernorm(x, axis=-1, eps=1e-05):
    m = jnp.mean(x, axis=axis, keepdims=True)
    v = jnp.var(x, axis=axis, keepdims=True)
    return (x - m) / jnp.sqrt(v + eps)

def _scatter_add(tgt, idx, src, axis=0):
    return tgt.at[idx].add(src)

def _segment_sum(src, seg, n):
    return jax.ops.segment_sum(src, seg, n)
kernel_name = 'mk_macaron_d1_jaxref_r8_d0baf5'

def setup_inputs(seed: int=0):
    np.random.seed(seed)
    _w = jnp.asarray

    def _L0_attn_setup():
        import jax, jax.numpy as jnp
        import numpy as np
        EMBED_DIM = 128
        LAMBDA_INIT = 0.8
        EPS = 1e-05
        key = jax.random.key(seed)
        ks = jax.random.split(key, 8)
        D = EMBED_DIM
        x = jax.random.normal(ks[0], (4, 256, D), dtype=jnp.float32)
        s = 1.0 / np.sqrt(D)
        w_q12 = jax.random.uniform(ks[1], (D, 2 * D), jnp.float32, -s, s)
        w_k12 = jax.random.uniform(ks[2], (D, 2 * D), jnp.float32, -s, s)
        w_v = jax.random.uniform(ks[3], (D, D), jnp.float32, -s, s)
        lambda_q1 = 0.1 * jax.random.normal(ks[4], (D,), jnp.float32)
        lambda_k1 = 0.1 * jax.random.normal(ks[5], (D,), jnp.float32)
        lambda_q2 = 0.1 * jax.random.normal(ks[6], (D,), jnp.float32)
        lambda_k2 = 0.1 * jax.random.normal(ks[7], (D,), jnp.float32)
        return {'x': x, 'w_q12': w_q12, 'w_k12': w_k12, 'w_v': w_v, 'lambda_q1': lambda_q1, 'lambda_k1': lambda_k1, 'lambda_q2': lambda_q2, 'lambda_k2': lambda_k2}
    _L0_attn_in = _L0_attn_setup()

    def _L0_ffn_setup():
        import jax, jax.numpy as jnp
        import numpy as np
        B, S, D, F, E = (2, 256, 128, 512, 8)
        LN_EPS = 1e-05

        def _layer_norm(x, gamma, beta):
            mu = jnp.mean(x, axis=-1, keepdims=True)
            var = jnp.mean(jnp.square(x - mu), axis=-1, keepdims=True)
            return (x - mu) * jax.lax.rsqrt(var + LN_EPS) * gamma + beta
        key = jax.random.key(seed)
        ks = jax.random.split(key, 8)

        def xavier(k, shape):
            fan_in, fan_out = (shape[-1], shape[-2])
            a = jnp.sqrt(6.0 / (fan_in + fan_out))
            return jax.random.uniform(k, shape, jnp.float32, -a, a)
        return {'tgt': jax.random.normal(ks[0], (B, S, D), jnp.float32), 'Wr': xavier(ks[1], (E, D)), 'br': jnp.zeros((E,), jnp.float32), 'W1': xavier(ks[2], (E, F, D)), 'b1': jnp.zeros((E, F), jnp.float32), 'W2': xavier(ks[3], (E, D, F)), 'b2': jnp.zeros((E, D), jnp.float32), 'gamma': jnp.ones((D,), jnp.float32), 'beta': jnp.zeros((D,), jnp.float32)}
    _L0_ffn_in = _L0_ffn_setup()
    _d = {'L0_attn_x': _L0_attn_in['x'], 'L0_attn_w_q12': _L0_attn_in['w_q12'], 'L0_attn_w_k12': _L0_attn_in['w_k12'], 'L0_attn_w_v': _L0_attn_in['w_v'], 'L0_attn_lambda_q1': _L0_attn_in['lambda_q1'], 'L0_attn_lambda_k1': _L0_attn_in['lambda_k1'], 'L0_attn_lambda_q2': _L0_attn_in['lambda_q2'], 'L0_attn_lambda_k2': _L0_attn_in['lambda_k2'], 'L0_ffn_Wr': _L0_ffn_in['Wr'], 'L0_ffn_br': _L0_ffn_in['br'], 'L0_ffn_W1': _L0_ffn_in['W1'], 'L0_ffn_b1': _L0_ffn_in['b1'], 'L0_ffn_W2': _L0_ffn_in['W2'], 'L0_ffn_b2': _L0_ffn_in['b2'], 'L0_ffn_gamma': _L0_ffn_in['gamma'], 'L0_ffn_beta': _L0_ffn_in['beta']}
    _x0 = _d['L0_attn_x']
    _d['L0_attn_x'] = jax.random.normal(jax.random.fold_in(jax.random.key(seed), 1), (4, 1024, 128), dtype=_x0.dtype)
    del _x0
    return _d

def reference(L0_attn_x, L0_attn_w_q12, L0_attn_w_k12, L0_attn_w_v, L0_attn_lambda_q1, L0_attn_lambda_k1, L0_attn_lambda_q2, L0_attn_lambda_k2, L0_ffn_Wr, L0_ffn_br, L0_ffn_W1, L0_ffn_b1, L0_ffn_W2, L0_ffn_b2, L0_ffn_gamma, L0_ffn_beta):

    def _L0_attn_ref(x, w_q12, w_k12, w_v, lambda_q1, lambda_k1, lambda_q2, lambda_k2):
        import jax, jax.numpy as jnp
        import numpy as np
        EMBED_DIM = 128
        LAMBDA_INIT = 0.8
        EPS = 1e-05
        D = x.shape[-1]
        scale = D ** (-0.25)
        q12 = jnp.einsum('bsd,de->bse', x, w_q12)
        k12 = jnp.einsum('bsd,de->bse', x, w_k12)
        q1, q2 = jnp.split(q12, 2, axis=-1)
        k1, k2 = jnp.split(k12, 2, axis=-1)
        v = jnp.einsum('bsd,de->bse', x, w_v)
        attn1 = jnp.einsum('bqd,bkd->bqk', q1, k1) * scale
        attn2 = jnp.einsum('bqd,bkd->bqk', q2, k2) * scale
        lam1 = jnp.exp(jnp.sum(lambda_q1 * lambda_k1))
        lam2 = jnp.exp(jnp.sum(lambda_q2 * lambda_k2))
        lam_full = lam1 - lam2 + LAMBDA_INIT
        diff = jax.nn.softmax(attn1, axis=-1) - lam_full * jax.nn.softmax(attn2, axis=-1)
        out = jnp.einsum('bqk,bkd->bqd', diff, v)
        rms = jnp.sqrt(jnp.mean(out * out, axis=-1, keepdims=True) + EPS)
        return out / rms * (1.0 - LAMBDA_INIT)

    def _L0_ffn_ref(tgt, Wr, br, W1, b1, W2, b2, gamma, beta):
        import jax, jax.numpy as jnp
        import numpy as np
        B, S, D, F, E = (2, 256, 128, 512, 8)
        LN_EPS = 1e-05

        def _layer_norm(x, gamma, beta):
            mu = jnp.mean(x, axis=-1, keepdims=True)
            var = jnp.mean(jnp.square(x - mu), axis=-1, keepdims=True)
            return (x - mu) * jax.lax.rsqrt(var + LN_EPS) * gamma + beta
        logits = jnp.einsum('bsd,ed->bse', tgt, Wr) + br
        top_v, top_i = jax.lax.top_k(logits, 2)
        top_w = jax.nn.softmax(top_v, axis=-1)
        n_exp = logits.shape[-1]
        router_w = jnp.sum(jax.nn.one_hot(top_i, n_exp, dtype=top_w.dtype) * top_w[..., None], axis=-2)
        h = jnp.einsum('bsd,efd->bsef', tgt, W1) + b1
        h = jax.nn.relu(h)
        o = jnp.einsum('bsef,edf->bsed', h, W2) + b2
        tgt2 = jnp.einsum('bsed,bse->bsd', o, router_w)
        return _layer_norm(tgt + tgt2, gamma, beta)
    x = L0_attn_x
    x = x + 0.5 * _L0_ffn_ref(_layernorm(x, axis=-1), L0_ffn_Wr, L0_ffn_br, L0_ffn_W1, L0_ffn_b1, L0_ffn_W2, L0_ffn_b2, L0_ffn_gamma, L0_ffn_beta)
    x = x + _L0_attn_ref(_layernorm(x, axis=-1), L0_attn_w_q12, L0_attn_w_k12, L0_attn_w_v, L0_attn_lambda_q1, L0_attn_lambda_k1, L0_attn_lambda_q2, L0_attn_lambda_k2)
    x = x + 0.5 * _L0_ffn_ref(_layernorm(x, axis=-1), L0_ffn_Wr, L0_ffn_br, L0_ffn_W1, L0_ffn_b1, L0_ffn_W2, L0_ffn_b2, L0_ffn_gamma, L0_ffn_beta)
    return x

_drawn_inputs = setup_inputs


def setup_inputs(seed=0):
    import zlib

    import numpy as np

    out = dict(_drawn_inputs(seed))
    spreads = {'L0_ffn_br': (0.0, 0.1),
     'L0_ffn_b1': (0.0, 0.1),
     'L0_ffn_b2': (0.0, 0.1),
     'L0_ffn_gamma': (1.0, 0.2),
     'L0_ffn_beta': (0.0, 0.1)}
    factors = {'L0_attn_lambda_q1': 200.0, 'L0_attn_lambda_q2': 200.0, 'L0_attn_lambda_k2': 3.747}
    for name, (base, spread) in spreads.items():
        noise = np.random.default_rng([zlib.crc32(name.encode()), seed]).standard_normal(out[name].shape)
        drawn = base * np.exp(spread * noise) if base else spread * noise
        out[name] = jnp.asarray(drawn.astype(out[name].dtype))
    for name, factor in factors.items():
        out[name] = (out[name] * factor).astype(out[name].dtype)
    return out
```

```python
import concourse.bass as bass
from concourse import mybir
from contextlib import ExitStack

F32 = mybir.dt.float32
F32R = mybir.dt.float32r
I32 = mybir.dt.int32
ALU = mybir.AluOpType
ACT = mybir.ActivationFunctionType
AX_X = mybir.AxisListType.X

P = 128


class Steps:

    def __init__(self, eng, sem):
        self.eng, self.sem, self.start, self.n = eng, sem, 0, 0

    def begin(self, start):
        self.start, self.n = start, 0

    def then(self, ins):
        ins.then_inc(self.sem, 1)
        self.n += 1
        self.eng.wait_ge(self.sem, self.start + self.n)


def macaron_kernel(nc, x_in, w_q12, w_k12, w_v, lq1, lk1, lq2, lk2, Wr, br, W1, b1, W2, b2, gamma, beta, out):
    BATCHES, S, D = x_in.shape
    E, F, _ = W1.shape
    TB = S // P
    NT = BATCHES * TB
    N = BATCHES * S
    FC = F // P
    PAIRS = 2 * TB
    REGION = N + P
    ROW = D + 1
    SLOTS = -(-(2 * N // P + E - 1) // 8) * 8
    RING = 8
    LAPS = SLOTS // RING
    EPS = 1e-5
    SCALE = float(D) ** -0.25
    LAMBDA_INIT = 0.8
    OUT_GAIN = (1.0 - LAMBDA_INIT) ** -2
    QG = 4
    assert D == P and S == TB * P and F % P == 0 and SLOTS % RING == 0 and TB % QG == 0
    assert SLOTS - 2 * N // P <= 8

    rows = nc.dram_tensor("rows", [E * REGION + P, ROW], F32).ap()
    results = nc.dram_tensor("results", [2 * N, D], F32).ap()

    ctx = ExitStack()
    with ctx:
        def sb(name, cols, dt=F32, parts=P):
            return ctx.enter_context(nc.sbuf_tensor(name, [parts, cols], dt))

        def sem(name):
            return ctx.enter_context(nc.semaphore(name))

        banks = ctx.enter_context(nc.psum_tensor("banks", [P, 8 * 512], F32))

        def bank(i, a=0, b=512):
            return banks[:, i * 512 + a:i * 512 + b]

        x = sb("x", NT * D)
        tgt = sb("tgt", NT * D)
        w1h, w1l = sb("w1h", E * F, F32R), sb("w1l", E * F, F32R)
        w2T = sb("w2T", E * FC * D)
        b1c = sb("b1c", E * FC)
        b2b = sb("b2b", E * D)
        gammab, betab = sb("gammab", D), sb("betab", D)
        brb = sb("brb", E)
        brt = sb("brt", E * TB)
        wrT = sb("wrT", E)
        wr, qkw, wv = tgt[0:E, 0:D], tgt[:, D:5 * D], tgt[:, 5 * D:6 * D]
        b1r = tgt[0:E * FC, 6 * D:7 * D]
        qkwh, qkwl = sb("qkwh", 4 * D, F32R), sb("qkwl", 4 * D, F32R)
        wvh, wvl = sb("wvh", D, F32R), sb("wvl", D, F32R)
        ident, ones, upper = sb("ident", P), sb("ones", P), sb("upper", P)
        lamv, lamp, lame, nlam = sb("lamv", 4), sb("lamp", 2), sb("lame", 2), sb("nlam", 1)
        nhalf = sb("nhalf", TB)
        st, mv, rs = sb("st", TB * 6), sb("mv", TB * 2), sb("rs", TB)
        rowbuf = sb("rowbuf", 2 * TB * 2 * ROW)
        dest = sb("dest", NT * 2, I32)
        tgtT = sb("tgtT", TB * P)
        G = E * TB
        lg, eq, oh1, oh2, cnt, pos, run = (sb(n, G) for n in ("lg", "eq", "oh1", "oh2", "cnt", "pos", "run"))
        first, segm = sb("first", G), sb("segm", G)
        m1, m2, kk, ex, den = (sb(n, TB) for n in ("m1", "m2", "kk", "ex", "den"))
        wts = sb("wts", NT * 2)
        slotf, slot = sb("slotf", 2 * TB), sb("slot", 2 * 2 * TB, I32)
        carry, base = sb("carry", E), sb("base", E)
        carry_i = sb("carry_i", E, I32)
        tile128 = sb("tile128", NT, parts=1)
        ntile, tend, onesE = sb("ntile", E, parts=1), sb("tend", E, parts=1), sb("onesE", E, parts=1)
        sidx = sb("sidx", SLOTS, parts=1)
        expert_of = sb("expert_of", SLOTS, I32, parts=1)
        row_of = sb("row_of", SLOTS, I32, parts=1)
        padrows = sb("padrows", ROW)
        xh, xl = sb("xh", 2 * P, F32R), sb("xl", 2 * P, F32R)
        zb = sb("zb", PAIRS * D)
        xn = sb("xn", TB * D)
        xnh, xnl = sb("xnh", S, F32R), sb("xnl", S, F32R)
        qkh, qkl = sb("qkh", 4 * S, F32R), sb("qkl", 4 * S, F32R)
        v = sb("v", TB * D)
        scratch = sb("scratch", 2 * 2 * S + TB * QG * P)
        p1 = [scratch[:, i * S:(i + 1) * S] for i in range(2)]
        p2 = [scratch[:, (2 + i) * S:(3 + i) * S] for i in range(2)]
        dT = scratch[:, 4 * S:4 * S + TB * QG * P]
        at = [0]

        def lent(n):
            at[0] += n
            return scratch[:, at[0] - n:at[0]]

        xt, hs, hT, ys = lent(RING * ROW), lent(2 * F), lent(2 * F), lent(RING * D)
        cmp1, cmp2 = lent(E * NT)[0:1, :], lent(SLOTS * E)[0:1, :]
        eidf, offf, roff = (lent(SLOTS)[0:1, :] for _ in range(3))
        raw1, raw2 = scratch[:, 0:E * F], scratch[:, E * F:2 * E * F]
        mx, nb = sb("mx", 2 * TB), sb("nb", 2 * TB)
        l1, l2 = sb("l1", TB), sb("l2", TB)
        r1, r2, cc = sb("r1", TB), sb("r2", TB), sb("cc", TB)
        oT, ob = xn[:, 0:QG * P], xn[:, QG * P:QG * (P + D)]
        sq = tgtT
        ss, so = sb("ss", TB), sb("so", TB)

        (x_loaded, w_loaded, small_loaded, masks_made, pool_step, dve_step, wT_ps, w_half, w1_sb, w2_sb, wr_ps,
         lam_in, lam_ps, lam_exp, ln_stats, ln_rstd, rows_ready, rows_copied, tgtT_ps, tgtT_sb, logits_ps,
         gap_ready, gap_exp, cnt_ready, prefix_ps, slots_ready, table_ready, pads_sent,
         xT_ps, xh_ready, xl_ready, h_ps, h_sb, hT_ps, hT_sb, y_ps, y_sb,
         z_used, xn_ready, xnT_ps, xnh_ready, xnl_ready, proj_ps, projh_ready, projl_ready,
         v_ps, v_sb, s_ps, nb_ready, p_ready, diff_ready, dT_ps, dT_sb, oT_ps, oT_sb, o_ps, ob_ready,
         ss_ready, so_ready, x_done, stored) = (sem(n) for n in (
            "x_loaded", "w_loaded", "small_loaded", "masks_made", "pool_step", "dve_step", "wT_ps", "w_half",
            "w1_sb", "w2_sb", "wr_ps", "lam_in", "lam_ps", "lam_exp", "ln_stats", "ln_rstd", "rows_ready",
            "rows_copied", "tgtT_ps", "tgtT_sb", "logits_ps", "gap_ready", "gap_exp", "cnt_ready",
            "prefix_ps", "slots_ready", "table_ready", "pads_sent", "xT_ps", "xh_ready",
            "xl_ready", "h_ps", "h_sb", "hT_ps", "hT_sb", "y_ps", "y_sb", "z_used", "xn_ready",
            "xnT_ps", "xnh_ready", "xnl_ready", "proj_ps", "projh_ready", "projl_ready", "v_ps", "v_sb",
            "s_ps", "nb_ready", "p_ready", "diff_ready", "dT_ps", "dT_sb", "oT_ps", "oT_sb", "o_ps",
            "ob_ready", "ss_ready", "so_ready", "x_done", "stored"))
        xt_loaded = [sem(f"xt_loaded{r}") for r in range(RING)]
        rows_sent = [sem(f"rows_sent{par}") for par in range(2)]
        went_by = sem("went_by")
        z_loaded = [sem(f"z_loaded{h}") for h in range(2)]
        y_sent = [sem(f"y_sent{r}") for r in range(RING)]

        def cols(t, i, n):
            return t[:, i * n:(i + 1) * n] if isinstance(i, int) else t[:, bass.ds(i * n, n)]

        x_v = x_in.rearrange("b (p j) d -> b p (j d)", p=P)
        out_v = out.rearrange("b (p j) d -> b p (j d)", p=P)
        results_v = results.rearrange("(b p j) d -> b p (j d)", p=P, b=BATCHES)
        rowbuf_v = rowbuf[:, :].rearrange("p (a j k r) -> p a j k r", a=2, j=TB, k=2)
        dest_v = dest[:, :].rearrange("p (t k) -> p t k", k=2)
        slot_v = slot[:, :].rearrange("p (a j k) -> p a j k", a=2, k=2)
        xt_v = xt.rearrange("p (r c) -> p r c", r=RING)

        def by_expert(t):
            return t[:, :].rearrange("p (e t) -> p e t", e=E)

        def by_tile(t):
            return t[:, :].rearrange("p (e t) -> p t e", e=E)

        def over_experts(t):
            return t[:, :].unsqueeze(2).broadcast_to([P, TB, E])

        def over_tiles(t):
            return t[:, :].unsqueeze(2).broadcast_to([P, E, TB])

        N_SMALL = 13

        def wait_apart(eng, *waits):
            for sem, v in waits:
                eng.wait_ge(sem, v)
            eng.sem_inc(went_by, 1)

        block = ctx.enter_context(nc.Block())

        @block.sync
        def _(sp):
            for b in range(BATCHES):
                sp.dma_start(x[:, b * TB * D:(b + 1) * TB * D], x_v[b]).then_inc(x_loaded, 16)
            sp.dma_start(raw2.rearrange("d (e f) -> d e f", e=E), W2.rearrange("e d f -> d e f")).then_inc(w_loaded, 16)

            def experts(p):
                if p == 0:
                    sp.wait_ge(masks_made, 1)
                    sp.dma_start(rows[E * REGION:, :], padrows[:, :]).then_inc(pads_sent, 16)
                sp.wait_ge(table_ready, p + 1)
                for e in range(E):
                    at = sp.value_load(carry_i[0:1, e:e + 1], min_val=0, max_val=E * REGION)
                    sp.dma_start(rows[bass.ds(at, P), :], padrows[:, :]).then_inc(pads_sent, 16)
                sp.wait_ge(pads_sent, 16 * (1 + E * (p + 1)))
                for par in range(2):
                    sp.wait_ge(rows_sent[par], 16 * PAIRS * BATCHES // 2 * (p + 1))

                def load(lap, r, again):
                    s = lap * RING + r
                    at = sp.value_load(row_of[0:1, bass.ds(s, 1)], min_val=0, max_val=E * REGION)
                    if again:
                        wait_apart(sp, (xT_ps, SLOTS * p + s - RING + 1))
                        wait_apart(sp, (y_sent[r], 16 * (LAPS * p + lap)))
                    sp.dma_start(xt[:, r * ROW:(r + 1) * ROW], rows[bass.ds(at, P), :]).then_inc(xt_loaded[r], 16)

                for r in range(RING):
                    load(0, r, p > 0)
                with sp.Fori(1, LAPS) as lap:
                    for r in range(RING):
                        load(lap, r, True)
                for r in range(RING):
                    sp.wait_ge(y_sent[r], 16 * LAPS * (p + 1))

            def load_results(p, b):
                for h in range(2):
                    n = 2 * (BATCHES * p + b) + h
                    if n >= 2:
                        sp.wait_ge(z_used, n - 1)
                    c = slice(h * TB * D, (h + 1) * TB * D)
                    sp.dma_start(zb[:, c], results_v[b][:, c]).then_inc(z_loaded[h], 16)

            experts(0)
            for b in range(BATCHES):
                load_results(0, b)
            experts(1)
            for b in range(BATCHES):
                load_results(1, b)
                if b:
                    sp.wait_ge(x_done, b)
                    sp.dma_start(out_v[b - 1], x[:, (b - 1) * TB * D:b * TB * D]).then_inc(stored, 16)
            sp.wait_ge(x_done, BATCHES)
            sp.dma_start(out_v[BATCHES - 1], x[:, (BATCHES - 1) * TB * D:]).then_inc(stored, 16)
            sp.wait_ge(stored, 16 * BATCHES)

        @block.gpsimd
        def _(pool):
            steps = Steps(pool, pool_step)
            pool.memset(ident[:, :], 0.0)
            pool.memset(upper[:, :], 1.0)
            pool.memset(ones[:, :], 1.0)
            pool.memset(nhalf[:, :], -0.5)
            pool.memset(onesE[:, :], 1.0)
            pool.memset(padrows[:, :], 0.0)
            pool.memset(segm[:, :], 1.0)
            pool.iota(dest[:, :], [[2 * S, BATCHES], [2, TB], [1, 2]], base=0, channel_multiplier=2 * TB)
            pool.iota(base[:, :], [[REGION, E]], base=0, channel_multiplier=0, allow_small_or_imprecise_dtypes=True)
            pool.iota(first[:, :], [[-1, E], [0, TB]], base=E, channel_multiplier=0, allow_small_or_imprecise_dtypes=True)
            pool.iota(tile128[:, :], [[P, NT]], base=0, channel_multiplier=0, allow_small_or_imprecise_dtypes=True)
            steps.then(pool.iota(sidx[:, :], [[1, SLOTS]], base=0, channel_multiplier=0, allow_small_or_imprecise_dtypes=True))
            pool.affine_select(out=ident[:, :], in_=ident[:, :], compare_op=ALU.not_equal, fill=1.0, base=0,
                               pattern=[[-1, P]], channel_multiplier=1)
            pool.affine_select(out=upper[:, :], in_=upper[:, :], compare_op=ALU.is_gt, fill=0.0, base=0,
                               pattern=[[1, P]], channel_multiplier=-1)
            pool.iota(padrows[:, D:ROW].bitcast(I32), [[0, 1]], base=2 * N, channel_multiplier=1)
            steps.then(pool.affine_select(out=by_expert(segm), in_=by_expert(segm), compare_op=ALU.not_equal, fill=0.0, base=0,
                                          pattern=[[0, E], [1, TB]], channel_multiplier=0))
            pool.nop().then_inc(masks_made, 1)

            def rstd(n):
                wait_apart(pool, (ln_stats, n + 1))
                steps.then(pool.tensor_scalar(rs[:, :], mv[:, :].rearrange("p (j c) -> p j c", c=2)[:, :, 1], EPS, 0.0, ALU.add, ALU.add))
                pool.tensor_tensor(rs[:, :], rs[:, :], nhalf[:, :], ALU.pow).then_inc(ln_rstd, 1)

            def scatter(p, b, par):
                wait_apart(pool, (slots_ready, BATCHES * p + b + 1), (rows_copied, BATCHES * p + b + 1))
                for j in range(TB):
                    for k in range(2):
                        pool.indirect_dma_start(rows, bass.IndirectOffsetOnAxis(slot_v[:, par, j, k:k + 1], 0),
                                                rowbuf_v[:, par, j, k, :], None).then_inc(rows_sent[par], 16)

            def experts(p):
                def send(lap, r):
                    wait_apart(pool, (y_sb, SLOTS * p + lap * RING + r + 1))
                    pool.indirect_dma_start(results, bass.IndirectOffsetOnAxis(xt_v[:, r, D:ROW].bitcast(I32), 0),
                                            ys[:, r * D:(r + 1) * D], None, bounds_check=2 * N - 1,
                                            oob_is_err=False).then_inc(y_sent[r], 16)
                with pool.Fori(0, LAPS) as lap:
                    for r in range(RING):
                        send(lap, r)

            def attention(b):
                for g in range(TB // QG):
                    wait_apart(pool, (ss_ready, (TB // QG) * b + g + 1))
                    part = slice(g * QG, (g + 1) * QG)
                    steps.then(pool.tensor_scalar(so[:, part], ss[:, part], OUT_GAIN / D, OUT_GAIN * EPS, ALU.mult, ALU.add))
                    pool.tensor_tensor(so[:, part], so[:, part], nhalf[:, 0:QG], ALU.pow).then_inc(so_ready, 1)

            with pool.Fori(0, BATCHES // 2) as half:
                for par in range(2):
                    b = half * 2 + par
                    steps.begin(2 + b)
                    rstd(b)
                    scatter(0, b, par)
            experts(0)
            with pool.Fori(0, BATCHES // 2) as half:
                for par in range(2):
                    b = half * 2 + par
                    steps.begin(2 + BATCHES + 5 * b)
                    rstd(BATCHES + 3 * b)
                    rstd(BATCHES + 3 * b + 1)
                    attention(b)
                    rstd(BATCHES + 3 * b + 2)
                    scatter(1, b, par)
            experts(1)
            with pool.Fori(0, BATCHES) as b:
                steps.begin(2 + 6 * BATCHES + b)
                rstd(4 * BATCHES + b)

        @block.scalar
        def _(act):
            act.dma_start(wr[:, :], Wr).then_inc(small_loaded, 16)
            act.dma_start(raw1.rearrange("f (g d) -> f g d", d=D), W1.rearrange("e (c f) d -> f (e c) d", f=P)).then_inc(w_loaded, 16)
            act.dma_start(brb[:, :], br.partition_broadcast(P)).then_inc(small_loaded, 16)
            act.dma_start(qkw[:, 0:2 * D], w_q12).then_inc(small_loaded, 16)
            act.dma_start(qkw[:, 2 * D:4 * D], w_k12).then_inc(small_loaded, 16)
            act.dma_start(wv[:, :], w_v).then_inc(small_loaded, 16)
            for i, l in enumerate((lq1, lk1, lq2, lk2)):
                act.dma_start(lamv[:, i:i + 1], l.rearrange("(d a) -> d a", a=1)).then_inc(small_loaded, 16)
            act.dma_start(gammab[:, :], gamma.partition_broadcast(P)).then_inc(small_loaded, 16)
            act.dma_start(betab[:, :], beta.partition_broadcast(P)).then_inc(small_loaded, 16)
            act.dma_start(b2b[:, :], b2.rearrange("e d -> (e d)").partition_broadcast(P)).then_inc(small_loaded, 16)
            act.dma_start(b1r, b1.rearrange("e (c f) -> (e c) f", f=P)).then_inc(small_loaded, 16)

            def setup():
                for g in range(E):
                    act.wait_ge(wT_ps, 2 * g + 1)
                    act.activation(w1h[:, g * F:(g + 1) * F], bank(g % 2), ACT.Copy).then_inc(w_half, 1)
                    act.wait_ge(wT_ps, 2 * g + 2)
                    act.activation(w2T[:, g * F:(g + 1) * F], bank(2 + g % 2), ACT.Copy).then_inc(w2_sb, 1)
                act.wait_ge(lam_ps, 1)
                act.activation(lame[:, :], bank(5, 0, 2), ACT.Exp).then_inc(lam_exp, 1)

            def route(p, b, par):
                a = BATCHES * p + b
                act.wait_ge(rows_ready, a + 1)
                rb = rowbuf_v[:, par, :, 0, 0:D]
                act.activation(rowbuf_v[:, par, :, 1, 0:D], rb, ACT.Copy)
                act.activation(cols(tgt, b, TB * D).rearrange("p (j d) -> p j d", j=TB), rb, ACT.Copy).then_inc(rows_copied, 1)
                for i in range(2):
                    act.wait_ge(tgtT_ps, 2 * a + i + 1)
                    act.activation(tgtT[:, i * 512:(i + 1) * 512], bank(6 + i), ACT.Copy).then_inc(tgtT_sb, 1)
                act.wait_ge(gap_ready, a + 1)
                act.activation(ex[:, :], ex[:, :], ACT.Exp).then_inc(gap_exp, 1)

            def experts(p):
                def xh_part(s, u):
                    g = SLOTS * p + s
                    act.wait_ge(xT_ps, g + 1)
                    if p or not isinstance(s, int) or s >= 2:
                        act.wait_ge(h_ps, g - 1)
                    act.activation(xh[:, (u % 2) * P:(u % 2 + 1) * P], bank(u % 2, 0, P), ACT.Copy).then_inc(xh_ready, 1)

                def h_copy(s, u):
                    g, k = SLOTS * p + s, u % 2
                    act.wait_ge(h_ps, g + 1)
                    if p or not isinstance(s, int) or s >= 2:
                        act.wait_ge(hT_ps, g - 1)
                    act.activation(hs[:, k * F:(k + 1) * F], bank(2 + k), ACT.Copy).then_inc(h_sb, 1)

                xh_part(0, 0)
                for s in range(2):
                    xh_part(s + 1, s + 1)
                    h_copy(s, s)
                with act.Fori(1, SLOTS // 2 - 1) as i:
                    for u in range(2):
                        xh_part(i * 2 + u + 1, u + 1)
                        h_copy(i * 2 + u, u)
                xh_part(SLOTS - 1, 1)
                h_copy(SLOTS - 2, 0)
                h_copy(SLOTS - 1, 1)

            def attention(b):
                for i in range(2):
                    act.wait_ge(xnT_ps, 2 * b + i + 1)
                    act.activation(xnh[:, i * 512:(i + 1) * 512], bank(6 + i), ACT.Copy).then_inc(xnh_ready, 1)
                for m in range(8):
                    act.wait_ge(proj_ps, 8 * b + m + 1)
                    act.activation(qkh[:, m * 512:(m + 1) * 512], bank(m % 4), ACT.Copy).then_inc(projh_ready, 1)
                for i in range(2):
                    act.wait_ge(v_ps, 2 * b + i + 1)
                    act.activation(v[:, i * 512:(i + 1) * 512], bank(4 + i), ACT.Copy).then_inc(v_sb, 1)

                def dT_copy(i):
                    act.wait_ge(dT_ps, TB * b + i + 1)
                    if i % QG == 0 and i:
                        act.wait_ge(oT_ps, (TB // QG) * b + i // QG)
                    act.activation(dT.rearrange("p (k q) -> p k q", k=TB)[:, :, (i % QG) * P:(i % QG + 1) * P],
                                   banks[:, 4 * 512:6 * 512].rearrange("p (k q) -> p k q", k=TB), ACT.Copy).then_inc(dT_sb, 1)

                def o_copy(g):
                    act.wait_ge(oT_ps, (TB // QG) * b + g + 1)
                    act.activation(oT[:, :], bank(6), ACT.Copy).then_inc(oT_sb, 1)

                def squares(g):
                    act.wait_ge(ob_ready, (TB // QG) * b + g + 1)
                    for q in range(QG):
                        i = g * QG + q
                        ins = act.activation(sq[:, i * D:(i + 1) * D], ob[:, q * D:(q + 1) * D], ACT.Square, accum_out=ss[:, i:i + 1])
                    ins.then_inc(ss_ready, 1)

                for i in range(TB):
                    for m, (pp, ll) in enumerate(((p1, l1), (p2, l2))):
                        act.wait_ge(nb_ready, 2 * (TB * b + i) + m + 1)
                        if i >= 2:
                            act.wait_ge(dT_ps, TB * b + i - 1)
                        act.activation(pp[i % 2], banks[:, 2 * m * 512:(2 * m + 2) * 512], ACT.Exp,
                                       bias=nb[:, 2 * i + m:2 * i + m + 1], scale=SCALE,
                                       accum_out=ll[:, i:i + 1]).then_inc(p_ready, 1)
                    if i:
                        dT_copy(i - 1)
                    if i == QG:
                        o_copy(0)
                    if i == QG + 1:
                        squares(0)
                dT_copy(TB - 1)
                o_copy(1)
                squares(1)

            setup()
            with act.Fori(0, BATCHES // 2) as half:
                for par in range(2):
                    route(0, half * 2 + par, par)
            experts(0)
            with act.Fori(0, BATCHES // 2) as half:
                for par in range(2):
                    attention(half * 2 + par)
                    route(1, half * 2 + par, par)
            experts(1)

        @block.tensor
        def _(pe):
            def three(o, ah, al, bh, bl, start=True, stop=True):
                pe.matmul(o, ah, bh, start=start, stop=False)
                pe.matmul(o, ah, bl, start=False, stop=False)
                return pe.matmul(o, al, bh, start=False, stop=stop)

            def setup():
                pe.wait_ge(masks_made, 1)
                pe.wait_ge(w_loaded, 32)
                for g in range(E):
                    if g >= 2:
                        pe.wait_ge(w1_sb, g - 1)
                        pe.wait_ge(w2_sb, g - 1)
                    for c in range(FC):
                        k = g * FC + c
                        ins = pe.transpose(bank(g % 2, c * P, (c + 1) * P), raw1[:, k * D:(k + 1) * D], ident[:, :])
                    ins.then_inc(wT_ps, 1)
                    for c in range(FC):
                        k = g * FC + c
                        ins = pe.transpose(bank(2 + g % 2, c * P, (c + 1) * P), raw2[:, k * P:(k + 1) * P], ident[:, :])
                    ins.then_inc(wT_ps, 1)
                pe.wait_ge(small_loaded, 16 * N_SMALL)
                pe.transpose(bank(4, 0, E), wr[:, :], ident[0:E, 0:E])
                pe.transpose(bank(4, E, E + E * FC), b1r, ident[0:E * FC, 0:E * FC]).then_inc(wr_ps, 1)
                pe.wait_ge(lam_in, 1)
                pe.matmul(bank(5, 0, 2), ones[:, :], lamp[:, :], start=True, stop=True).then_inc(lam_ps, 1)

            def route(p, b, par):
                a = BATCHES * p + b
                pe.wait_ge(rows_ready, a + 1)
                for i in range(2):
                    for j in range(4):
                        ins = pe.transpose(bank(6 + i, j * P, (j + 1) * P), rowbuf_v[:, par, 4 * i + j, 0, 0:D], ident[:, :])
                    ins.then_inc(tgtT_ps, 1)
                pe.wait_ge(tgtT_sb, 2 * a + 2)
                lo = bank(7, 0, G).rearrange("p (e t) -> p e t", e=E)
                for j in range(TB):
                    ins = pe.matmul(lo[:, :, j], tgtT[:, j * P:(j + 1) * P], wrT[:, :], start=True, stop=True)
                ins.then_inc(logits_ps, 1)
                pe.wait_ge(cnt_ready, a + 1)
                pe.matmul(bank(6, 0, G), upper[:, :], cnt[:, :], start=True, stop=True)
                pe.matmul(bank(6, G, 2 * G), ones[:, :], cnt[:, :], start=True, stop=True).then_inc(prefix_ps, 1)

            def experts(p):
                def later(s, n):
                    return p > 0 or not isinstance(s, int) or s >= n

                def turn_x(s, u):
                    g, r = SLOTS * p + s, u % RING
                    lap = s // RING if isinstance(s, int) else s_lap[0] + u // RING
                    pe.wait_ge(xt_loaded[r], 16 * (LAPS * p + lap + 1))
                    if later(s, 2):
                        pe.wait_ge(xl_ready, g - 1)
                    pe.transpose(bank(u % 2, 0, P), xt_v[:, r, 0:D], ident[:, :]).then_inc(xT_ps, 1)

                def first(s, u):
                    g, k = SLOTS * p + s, u % 2
                    e = pe.value_load(expert_of[0:1, bass.ds(s, 1)], min_val=0, max_val=E - 1)
                    pe.wait_ge(xl_ready, g + 1)
                    if later(s, 2):
                        pe.wait_ge(h_sb, g - 1)
                    three(bank(2 + k), xh[:, k * P:(k + 1) * P], xl[:, k * P:(k + 1) * P],
                          w1h[:, bass.ds(e * F, F)], w1l[:, bass.ds(e * F, F)]).then_inc(h_ps, 1)

                def turn_h(s, u):
                    g, k = SLOTS * p + s, u % 2
                    pe.wait_ge(h_sb, g + 1)
                    if later(s, 2):
                        pe.wait_ge(hT_sb, g - 1)
                    for c in range(FC):
                        ins = pe.transpose(bank(4 + k, c * P, (c + 1) * P), hs[:, k * F + c * P:k * F + (c + 1) * P], ident[:, :])
                    ins.then_inc(hT_ps, 1)

                def second(s, u):
                    g, k = SLOTS * p + s, u % 2
                    e = pe.value_load(expert_of[0:1, bass.ds(s, 1)], min_val=0, max_val=E - 1)
                    pe.wait_ge(hT_sb, g + 1)
                    if later(s, 2):
                        pe.wait_ge(y_sb, g - 1)
                    for c in range(FC):
                        ins = pe.matmul(bank(6 + k, 0, D), hT[:, k * F + c * P:k * F + (c + 1) * P],
                                        w2T[:, bass.ds(e * F + c * D, D)], start=(c == 0), stop=(c == FC - 1))
                    ins.then_inc(y_ps, 1)

                def step(s, u):
                    known = isinstance(s, int)
                    if not known or s + 2 < SLOTS:
                        turn_x(s + 2, u + 2)
                    if not known or 0 <= s + 1 < SLOTS:
                        first(s + 1, u + 1)
                    if not known or 0 <= s < SLOTS:
                        turn_h(s, u)
                    if not known or s >= 1:
                        second(s - 1, u - 1)

                s_lap = [0]
                for s in range(-2, 3):
                    step(s, s)
                with pe.Fori(0, LAPS - 1) as lap:
                    s_lap[0] = lap
                    for u in range(3, RING + 3):
                        step(lap * RING + u, u)
                for s in range((LAPS - 1) * RING + 3, SLOTS + 1):
                    step(s, s)

            def attention(b):
                pe.wait_ge(xn_ready, b + 1)
                for i in range(2):
                    for j in range(4):
                        t = 4 * i + j
                        ins = pe.transpose(bank(6 + i, j * P, (j + 1) * P), xn[:, t * D:(t + 1) * D], ident[:, :])
                    ins.then_inc(xnT_ps, 1)
                pe.wait_ge(xnl_ready, 2 * b + 2)
                for m in range(8):
                    w, h = slice((m // 2) * D, (m // 2 + 1) * D), slice((m % 2) * 512, (m % 2 + 1) * 512)
                    if m >= 4:
                        pe.wait_ge(projl_ready, 8 * b + m - 3)
                    three(bank(m % 4), qkwh[:, w], qkwl[:, w], xnh[:, h], xnl[:, h]).then_inc(proj_ps, 1)
                for i in range(2):
                    for j in range(4):
                        t = slice((4 * i + j) * P, (4 * i + j + 1) * P)
                        ins = three(bank(4 + i, j * P, (j + 1) * P), xnh[:, t], xnl[:, t], wvh[:, :], wvl[:, :])
                    ins.then_inc(v_ps, 1)

                def scores(i):
                    for m in range(2):
                        q = slice(m * S + i * P, m * S + (i + 1) * P)
                        if i:
                            pe.wait_ge(p_ready, 2 * (TB * b + i) + m - 1)
                        for h in range(2):
                            k = slice((2 + m) * S + h * 512, (2 + m) * S + (h + 1) * 512)
                            ins = three(bank(2 * m + h), qkh[:, q], qkl[:, q], qkh[:, k], qkl[:, k])
                        ins.then_inc(s_ps, 1)

                def turn(i):
                    pe.wait_ge(diff_ready, TB * b + i + 1)
                    if i:
                        pe.wait_ge(dT_sb, TB * b + i)
                    else:
                        pe.wait_ge(v_sb, 2 * b + 2)
                    for k in range(TB):
                        ins = pe.transpose(bank(4 + k // 4, (k % 4) * P, (k % 4 + 1) * P), p1[i % 2][:, k * P:(k + 1) * P], ident[:, :])
                    ins.then_inc(dT_ps, 1)

                def values(g):
                    pe.wait_ge(dT_sb, TB * b + (g + 1) * QG)
                    for k in range(TB):
                        ins = pe.matmul(bank(6), v[:, k * D:(k + 1) * D], dT[:, k * QG * P:(k + 1) * QG * P],
                                        start=(k == 0), stop=(k == TB - 1))
                    ins.then_inc(oT_ps, 1)

                def turn_back(g):
                    pe.wait_ge(oT_sb, (TB // QG) * b + g + 1)
                    if g:
                        pe.wait_ge(ob_ready, (TB // QG) * b + g)
                    for q in range(QG):
                        ins = pe.transpose(bank(7, q * P, (q + 1) * P), oT[:, q * P:(q + 1) * P], ident[:, :])
                    ins.then_inc(o_ps, 1)

                pe.wait_ge(projl_ready, 8 * b + 8)
                for i in range(TB):
                    scores(i)
                    if i:
                        turn(i - 1)
                    if i == QG:
                        values(0)
                    if i == QG + 1:
                        turn_back(0)
                turn(TB - 1)
                values(1)
                turn_back(1)

            setup()
            pe.wait_ge(w1_sb, E)
            pe.wait_ge(w2_sb, E)
            with pe.Fori(0, BATCHES // 2) as half:
                for par in range(2):
                    route(0, half * 2 + par, par)
            pe.wait_ge(table_ready, 1)
            experts(0)
            with pe.Fori(0, BATCHES // 2) as half:
                for par in range(2):
                    attention(half * 2 + par)
                    route(1, half * 2 + par, par)
            pe.wait_ge(table_ready, 2)
            experts(1)

        @block.vector
        def _(dve):
            steps = Steps(dve, dve_step)

            def setup():
                dve.wait_ge(masks_made, 1)
                for g in range(E):
                    dve.wait_ge(w_half, g + 1)
                    dve.tensor_tensor(w1l[:, g * F:(g + 1) * F], bank(g % 2), w1h[:, g * F:(g + 1) * F].bitcast(F32),
                                      ALU.subtract).then_inc(w1_sb, 1)
                dve.wait_ge(wr_ps, 1)
                dve.tensor_copy(wrT[:, :], bank(4, 0, E))
                dve.tensor_copy(b1c[:, :], bank(4, E, E + E * FC))
                dve.tensor_copy(by_expert(brt), over_tiles(brb))
                dve.tensor_copy(carry[:, :], base[:, :])
                dve.tensor_copy(qkwh[:, :], qkw[:, :])
                dve.tensor_copy(wvh[:, :], wv[:, :])
                dve.tensor_scalar(gammab[:, :], gammab[:, :], 0.5, None, ALU.mult)
                dve.tensor_scalar(betab[:, :], betab[:, :], 0.5, None, ALU.mult)
                dve.tensor_tensor(lamp[:, 0:1], lamv[:, 0:1], lamv[:, 1:2], ALU.mult)
                steps.then(dve.tensor_tensor(lamp[:, 1:2], lamv[:, 2:3], lamv[:, 3:4], ALU.mult))
                dve.tensor_tensor(qkwl[:, :], qkw[:, :], qkwh[:, :].bitcast(F32), ALU.subtract).then_inc(lam_in, 1)
                dve.tensor_tensor(wvl[:, :], wv[:, :], wvh[:, :].bitcast(F32), ALU.subtract)
                dve.wait_ge(lam_exp, 1)
                steps.then(dve.tensor_tensor(nlam[:, :], lame[:, 1:2], lame[:, 0:1], ALU.subtract))
                steps.then(dve.tensor_scalar(nlam[:, :], nlam[:, :], -LAMBDA_INIT, None, ALU.add))

            def stats(src, n):
                for j in range(TB):
                    ins = dve.bn_stats(st[:, j * 6:(j + 1) * 6], src(j))
                ins.then_inc(dve_step, 1)
                steps.n += 1
                wait_apart(dve, (dve_step, steps.start + steps.n))
                for j in range(TB):
                    ins = dve.bn_aggr(mv[:, j * 2:(j + 1) * 2], st[:, j * 6:(j + 1) * 6])
                ins.then_inc(ln_stats, 1)
                dve.wait_ge(ln_rstd, n + 1)

            def normalise(dst, src):
                for j in range(TB):
                    ins = dve.tensor_scalar(dst(j), src(j), mv[:, 2 * j:2 * j + 1], rs[:, j:j + 1], ALU.subtract, ALU.mult)
                return ins

            def route(p, b, half, par, n):
                a = BATCHES * p + b
                wait_apart(dve, (dve_step, steps.start + steps.n))
                stats(lambda j: cols(x, b * TB + j, D), n)
                if not isinstance(half, int) or half:
                    dve.wait_ge(rows_sent[par], 16 * PAIRS * (BATCHES // 2 * p + half))
                normalise(lambda j: rowbuf_v[:, par, j, 0, 0:D], lambda j: cols(x, b * TB + j, D))
                dve.tensor_copy(rowbuf_v[:, par, :, :, D].bitcast(I32),
                                dest_v[:, b * TB:(b + 1) * TB, :] if isinstance(b, int) else dest_v[:, bass.ds(b * TB, TB), :]).then_inc(rows_ready, 1)
                dve.wait_ge(logits_ps, a + 1)
                steps.then(dve.tensor_tensor(lg[:, :], bank(7, 0, G), brt[:, :], ALU.add))
                for m, oh in ((m1, oh1), (m2, oh2)):
                    steps.then(dve.tensor_reduce(m[:, :], by_tile(lg), AX_X, ALU.max))
                    steps.then(dve.tensor_tensor(by_tile(eq), by_tile(lg), over_experts(m), ALU.is_equal))
                    steps.then(dve.tensor_tensor(eq[:, :], eq[:, :], first[:, :], ALU.mult))
                    steps.then(dve.tensor_reduce(kk[:, :], by_tile(eq), AX_X, ALU.max))
                    steps.then(dve.tensor_tensor(by_tile(oh), by_tile(eq), over_experts(kk), ALU.is_equal))
                    if oh is oh1:
                        steps.then(dve.scalar_tensor_tensor(lg[:, :], oh1[:, :], -3.0e38, lg[:, :], ALU.mult, ALU.add))
                dve.tensor_tensor(cnt[:, :], oh1[:, :], oh2[:, :], ALU.add).then_inc(cnt_ready, 1)
                dve.tensor_tensor(ex[:, :], m2[:, :], m1[:, :], ALU.subtract).then_inc(gap_ready, 1)
                dve.wait_ge(gap_exp, a + 1)
                steps.then(dve.tensor_scalar(den[:, :], ex[:, :], 1.0, None, ALU.add))
                w = cols(wts, b, 2 * TB).rearrange("p (t k) -> p t k", k=2)
                steps.then(dve.reciprocal(den[:, :], den[:, :]))
                dve.tensor_copy(w[:, :, 0], den[:, :])
                dve.tensor_tensor(w[:, :, 1], ex[:, :], den[:, :], ALU.mult)
                dve.wait_ge(prefix_ps, a + 1)
                steps.then(dve.tensor_tensor_scan(run[:, :], segm[:, :], bank(6, G, 2 * G), 0.0, ALU.mult, ALU.add))
                steps.then(dve.tensor_tensor(pos[:, :], run[:, :], bank(6, G, 2 * G), ALU.subtract))
                steps.then(dve.tensor_tensor(pos[:, :], pos[:, :], bank(6, 0, G), ALU.add))
                steps.then(dve.tensor_tensor(by_expert(pos), by_expert(pos), over_tiles(carry), ALU.add))
                steps.then(dve.tensor_tensor(carry[:, :], carry[:, :], by_expert(run)[:, :, TB - 1], ALU.add))
                sv = slotf[:, :].rearrange("p (t k) -> p t k", k=2)
                for k, oh in enumerate((oh1, oh2)):
                    steps.then(dve.tensor_tensor(eq[:, :], oh[:, :], pos[:, :], ALU.mult))
                    steps.then(dve.tensor_reduce(sv[:, :, k], by_tile(eq), AX_X, ALU.add))
                dve.tensor_copy(slot[:, par * 2 * TB:(par + 1) * 2 * TB], slotf[:, :]).then_inc(slots_ready, 1)

            def table():
                dve.tensor_copy(carry_i[:, :], carry[:, :])
                steps.then(dve.tensor_tensor(carry[:, :], carry[:, :], base[:, :], ALU.subtract))
                c1 = cmp1[:, :].rearrange("p (e t) -> p e t", e=E)
                steps.then(dve.tensor_tensor(c1, carry[0:1, :].unsqueeze(2).broadcast_to([1, E, NT]),
                                             tile128[:, :].unsqueeze(1).broadcast_to([1, E, NT]), ALU.is_gt))
                steps.then(dve.tensor_reduce(ntile[:, :], c1, AX_X, ALU.add))
                steps.then(dve.tensor_tensor_scan(tend[:, :], onesE[:, :], ntile[:, :], 0.0, ALU.mult, ALU.add))
                c2 = cmp2[:, :].rearrange("p (s e) -> p s e", e=E)
                steps.then(dve.tensor_tensor(c2, sidx[:, :].unsqueeze(2).broadcast_to([1, SLOTS, E]),
                                             tend[:, :].unsqueeze(1).broadcast_to([1, SLOTS, E]), ALU.is_ge))
                steps.then(dve.tensor_reduce(eidf[:, :], c2, AX_X, ALU.add))
                steps.then(dve.tensor_tensor(c2, c2, ntile[:, :].unsqueeze(1).broadcast_to([1, SLOTS, E]), ALU.mult))
                steps.then(dve.tensor_reduce(offf[:, :], c2, AX_X, ALU.add))
                steps.then(dve.tensor_tensor(offf[:, :], sidx[:, :], offf[:, :], ALU.subtract))
                steps.then(dve.tensor_scalar(offf[:, :], offf[:, :], float(P), None, ALU.mult))
                steps.then(dve.scalar_tensor_tensor(roff[:, :], eidf[:, :], float(REGION), offf[:, :], ALU.mult, ALU.add))
                dve.tensor_scalar(row_of[:, :], roff[:, :], float(E * REGION), None, ALU.min)
                steps.then(dve.tensor_scalar(expert_of[:, :], eidf[:, :], float(E - 1), None, ALU.min))
                dve.tensor_copy(carry[:, :], base[:, :]).then_inc(table_ready, 1)

            TABLE = 12

            def experts(p):
                def later(s, n):
                    return p > 0 or not isinstance(s, int) or s >= n

                def x_rest(s, u):
                    g, k = SLOTS * p + s, u % 2
                    dve.wait_ge(xh_ready, g + 1)
                    dve.tensor_tensor(xl[:, k * P:(k + 1) * P], bank(k, 0, P), xh[:, k * P:(k + 1) * P].bitcast(F32),
                                      ALU.subtract).then_inc(xl_ready, 1)

                def relu(s, u):
                    g, k = SLOTS * p + s, u % 2
                    e = dve.value_load(expert_of[0:1, bass.ds(s, 1)], min_val=0, max_val=E - 1)
                    dve.wait_ge(hT_ps, g + 1)
                    if later(s, 2):
                        dve.wait_ge(y_ps, g - 1)
                    for c in range(FC):
                        ins = dve.tensor_scalar(hT[:, k * F + c * P:k * F + (c + 1) * P], bank(4 + k, c * P, (c + 1) * P),
                                                b1c[:, bass.ds(e * FC + c, 1)], 0.0, ALU.add, ALU.max)
                    ins.then_inc(hT_sb, 1)

                def add_b2(s, u):
                    g, k, r = SLOTS * p + s, u % 2, u % RING
                    lap = s // RING if isinstance(s, int) else s_lap[0] + u // RING
                    e = dve.value_load(expert_of[0:1, bass.ds(s, 1)], min_val=0, max_val=E - 1)
                    dve.wait_ge(y_ps, g + 1)
                    if later(s, RING):
                        dve.wait_ge(y_sent[r], 16 * (LAPS * p + lap))
                    dve.tensor_tensor(ys[:, r * D:(r + 1) * D], bank(6 + k, 0, D), b2b[:, bass.ds(e * D, D)], ALU.add).then_inc(y_sb, 1)

                def step(s, u):
                    known = isinstance(s, int)
                    if not known or s + 2 < SLOTS:
                        x_rest(s + 2, u + 2)
                    if not known or 0 <= s < SLOTS:
                        relu(s, u)
                    if not known or s >= 1:
                        add_b2(s - 1, u - 1)

                s_lap = [0]
                for s in range(-2, RING + 3):
                    step(s, s)
                with dve.Fori(1, LAPS - 1) as lap:
                    s_lap[0] = lap
                    for u in range(3, RING + 3):
                        step(lap * RING + u, u)
                for s in range((LAPS - 1) * RING + 3, SLOTS + 1):
                    step(s, s)

            def merge(p, b, par, n):
                def z(j, k):
                    at = 2 * j + k
                    return zb[:, at * D:(at + 1) * D]

                def r(j):
                    return xn[:, j * D:(j + 1) * D]

                def w(j, k):
                    return cols(wts, (b * TB + j) * 2 + k, 1)

                for h in range(2):
                    dve.wait_ge(z_loaded[h], 16 * (BATCHES * p + b + 1))
                    js = range(h * TB // 2, (h + 1) * TB // 2)
                    for j in js:
                        ins = dve.scalar_tensor_tensor(r(j), z(j, 0), w(j, 0), cols(tgt, b * TB + j, D), ALU.mult, ALU.add)
                    steps.then(ins)
                    for j in js:
                        ins = dve.scalar_tensor_tensor(r(j), z(j, 1), w(j, 1), r(j), ALU.mult, ALU.add)
                    ins.then_inc(z_used, 1)
                dve.wait_ge(z_used, 2 * (BATCHES * p + b + 1))
                stats(r, n)
                steps.then(normalise(r, r))
                xb = cols(x, b, TB * D).rearrange("p (j d) -> p j d", j=TB)
                rb = xn[:, :].rearrange("p (j d) -> p j d", j=TB)
                steps.then(dve.tensor_tensor(rb, rb, gammab[:, :].unsqueeze(1).broadcast_to([P, TB, D]), ALU.mult))
                steps.then(dve.tensor_tensor(rb, rb, betab[:, :].unsqueeze(1).broadcast_to([P, TB, D]), ALU.add))
                ins = dve.tensor_tensor(xb, xb, rb, ALU.add)
                if p:
                    ins.then_inc(x_done, 1)
                    dve.wait_ge(x_done, b + 1)
                else:
                    steps.then(ins)

            def attention(b, n):
                wait_apart(dve, (dve_step, steps.start + steps.n))
                stats(lambda j: cols(x, b * TB + j, D), n)
                normalise(lambda j: xn[:, j * D:(j + 1) * D], lambda j: cols(x, b * TB + j, D)).then_inc(xn_ready, 1)
                for i in range(2):
                    h = slice(i * 512, (i + 1) * 512)
                    dve.wait_ge(xnh_ready, 2 * b + i + 1)
                    dve.tensor_tensor(xnl[:, h], bank(6 + i), xnh[:, h].bitcast(F32), ALU.subtract).then_inc(xnl_ready, 1)
                for m in range(8):
                    h = slice(m * 512, (m + 1) * 512)
                    dve.wait_ge(projh_ready, 8 * b + m + 1)
                    dve.tensor_tensor(qkl[:, h], bank(m % 4), qkh[:, h].bitcast(F32), ALU.subtract).then_inc(projl_ready, 1)

                def maxima(i):
                    for m in range(2):
                        c = slice(2 * i + m, 2 * i + m + 1)
                        dve.wait_ge(s_ps, 2 * (TB * b + i) + m + 1)
                        steps.then(dve.tensor_reduce(mx[:, c], banks[:, 2 * m * 512:(2 * m + 2) * 512], AX_X, ALU.max))
                        dve.tensor_scalar(nb[:, c], mx[:, c], -SCALE, None, ALU.mult).then_inc(nb_ready, 1)

                def difference(i):
                    c = slice(i, i + 1)
                    dve.wait_ge(p_ready, 2 * (TB * b + i) + 2)
                    dve.reciprocal(r1[:, c], l1[:, c])
                    steps.then(dve.reciprocal(r2[:, c], l2[:, c]))
                    steps.then(dve.tensor_scalar(cc[:, c], l1[:, c], r2[:, c], nlam[:, 0:1], ALU.mult, ALU.mult))
                    dve.scalar_tensor_tensor(p1[i % 2], p2[i % 2], cc[:, c], p1[i % 2], ALU.mult, ALU.add).then_inc(diff_ready, 1)

                def scale_values(g):
                    dve.wait_ge(o_ps, (TB // QG) * b + g + 1)
                    for q in range(QG):
                        i = g * QG + q
                        ins = dve.tensor_scalar(ob[:, q * D:(q + 1) * D], bank(7, q * P, (q + 1) * P), r1[:, i:i + 1], None, ALU.mult)
                    ins.then_inc(ob_ready, 1)

                def add_values(g):
                    dve.wait_ge(so_ready, (TB // QG) * b + g + 1)
                    for q in range(QG):
                        i = g * QG + q
                        xi = cols(x, b * TB + i, D)
                        ins = dve.scalar_tensor_tensor(xi, ob[:, q * D:(q + 1) * D], so[:, i:i + 1], xi, ALU.mult, ALU.add)
                    steps.then(ins)

                for i in range(TB):
                    maxima(i)
                    if i:
                        difference(i - 1)
                    if i == QG + 1:
                        scale_values(0)
                    if i == QG + 2:
                        add_values(0)
                difference(TB - 1)
                scale_values(1)
                add_values(1)

            setup()
            at = steps.n
            dve.wait_ge(x_loaded, 16 * BATCHES)
            R_, M_, A_ = 24, 7, 35
            for b in range(BATCHES):
                steps.begin(at + b * R_)
                route(0, b, b // 2, b % 2, b)
                assert steps.n == R_, steps.n
            at += BATCHES * R_
            steps.begin(at)
            table()
            at += TABLE
            assert steps.n == TABLE, steps.n
            experts(0)
            with dve.Fori(0, BATCHES // 2) as half:
                for par in range(2):
                    b = half * 2 + par
                    steps.begin(at + b * (M_ + A_ + R_))
                    merge(0, b, par, BATCHES + 3 * b)
                    assert steps.n == M_, steps.n
                    attention(b, BATCHES + 3 * b + 1)
                    assert steps.n == M_ + A_, steps.n
                    route(1, b, half, par, BATCHES + 3 * b + 2)
            at += BATCHES * (M_ + A_ + R_)
            steps.begin(at)
            table()
            at += TABLE
            experts(1)
            with dve.Fori(0, BATCHES // 2) as half:
                for par in range(2):
                    b = half * 2 + par
                    steps.begin(at + b * (M_ - 1))
                    merge(1, b, par, 4 * BATCHES + b)


_INS = ['L0_attn_x', 'L0_attn_w_q12', 'L0_attn_w_k12', 'L0_attn_w_v', 'L0_attn_lambda_q1', 'L0_attn_lambda_k1',
        'L0_attn_lambda_q2', 'L0_attn_lambda_k2', 'L0_ffn_Wr', 'L0_ffn_br', 'L0_ffn_W1', 'L0_ffn_b1', 'L0_ffn_W2',
        'L0_ffn_b2', 'L0_ffn_gamma', 'L0_ffn_beta']
_OUTS = [((4, 1024, 128), 'float32')]


def kernel(**inputs):
    import numpy as _np
    import concourse.bacc as _bacc
    from concourse import mybir as _mybir
    from concourse.bass_utils import run_bass_kernel_spmd as _run

    nc = _bacc.Bacc("TRN2", target_bir_lowering=False, num_devices=1)
    arrays, args = {}, []
    for name in _INS:
        a = _np.ascontiguousarray(inputs[name])
        arrays[f"in_{name}_dram"] = a
        args.append(nc.dram_tensor(f"in_{name}_dram", a.shape, _mybir.dt.from_np(a.dtype), kind="ExternalInput").ap())
    for i, (shape, dtype) in enumerate(_OUTS):
        dt = _mybir.dt.from_np(_np.dtype(dtype))
        args.append(nc.dram_tensor(f"out_{i}_dram", shape, dt, kind="ExternalOutput").ap())
    macaron_kernel(nc, *args)
    r = _run(nc, [arrays], core_ids=[0])
    return r.results[0]["out_0_dram"]
```

```python
import concourse.bass as bass
from concourse import mybir
from contextlib import ExitStack

F32 = mybir.dt.float32
F32R = mybir.dt.float32r
I32 = mybir.dt.int32
ALU = mybir.AluOpType
ACT = mybir.ActivationFunctionType
AX_X = mybir.AxisListType.X
PE, DVE = mybir.EngineType.PE, mybir.EngineType.DVE

P = 128


class Steps:

    def __init__(self, eng, sem):
        self.eng, self.sem, self.start, self.n = eng, sem, 0, 0

    def begin(self, start):
        self.start, self.n = start, 0

    def then(self, ins):
        ins.then_inc(self.sem, 1)
        self.n += 1
        self.eng.wait_ge(self.sem, self.start + self.n)


def macaron_kernel(nc, x_in, w_q12, w_k12, w_v, lq1, lk1, lq2, lk2, Wr, br, W1, b1, W2, b2, gamma, beta, out):
    BATCHES, S, D = x_in.shape
    E, F, _ = W1.shape
    TB = S // P
    NT = BATCHES * TB
    N = BATCHES * S
    FC = F // P
    PAIRS = 2 * TB
    REGION = N + P
    ROW = D + 1
    SLOTS = -(-(2 * N // P + E - 1) // 8) * 8
    RING = 8
    LAPS = SLOTS // RING
    EPS = 1e-5
    SCALE = float(D) ** -0.25
    LAMBDA_INIT = 0.8
    OUT_GAIN = (1.0 - LAMBDA_INIT) ** -2
    QG = 4
    assert D == P and S == TB * P and F % P == 0 and SLOTS % RING == 0 and TB % QG == 0
    assert SLOTS - 2 * N // P <= 8

    rows = nc.dram_tensor("rows", [E * REGION + P, ROW], F32).ap()
    results = nc.dram_tensor("results", [2 * N, D], F32).ap()

    ctx = ExitStack()
    with ctx:
        def sb(name, cols, dt=F32, parts=P):
            return ctx.enter_context(nc.sbuf_tensor(name, [parts, cols], dt))

        def sem(name):
            return ctx.enter_context(nc.semaphore(name))

        banks = ctx.enter_context(nc.psum_tensor("banks", [P, 8 * 512], F32))

        def bank(i, a=0, b=512):
            return banks[:, i * 512 + a:i * 512 + b]

        x = sb("x", NT * D)
        tgt = sb("tgt", NT * D)
        w1h, w1l = sb("w1h", E * F, F32R), sb("w1l", E * F, F32R)
        w2T = sb("w2T", E * FC * D)
        BIAS = FC + D
        biases = sb("biases", E * BIAS)
        gammab, betab = sb("gammab", D), sb("betab", D)
        brb = sb("brb", E)
        brt = sb("brt", E * TB)
        wrT = sb("wrT", E)
        wr = tgt[0:E, 0:D]
        b1r = tgt[0:E * FC, 6 * D:7 * D]
        qkw, wv = sb("qkw", 4 * D), sb("wv", D)
        ident, ones, upper = sb("ident", P), sb("ones", P), sb("upper", P)
        lamv, lamp, lame, nlam = sb("lamv", 4), sb("lamp", 2), sb("lame", 2), sb("nlam", 1)
        nhalf = sb("nhalf", TB)
        st_x, st_r = sb("st_x", TB * 6), sb("st_r", TB * 6)
        mv2, rs2 = sb("mv", 2 * TB * 2), sb("rs", 2 * TB)
        rowbuf = sb("rowbuf", 2 * TB * 2 * ROW)
        dest = sb("dest", NT * 2, I32)
        tgtT = sb("tgtT", TB * P)
        G = E * TB
        lg, eq, oh1, oh2, cnt, pos, run = (sb(n, G) for n in ("lg", "eq", "oh1", "oh2", "cnt", "pos", "run"))
        first, segm = sb("first", G), sb("segm", G)
        m1, m2, kk, ex, den = (sb(n, TB) for n in ("m1", "m2", "kk", "ex", "den"))
        wts = sb("wts", NT * 2)
        slotf, slot = sb("slotf", 2 * TB), sb("slot", 2 * 2 * TB, I32)
        carry, base = sb("carry", E), sb("base", E)
        carry_i = sb("carry_i", E, I32)
        tile128 = sb("tile128", NT, parts=1)
        ntile, tend, onesE = sb("ntile", E, parts=1), sb("tend", E, parts=1), sb("onesE", E, parts=1)
        sidx = sb("sidx", SLOTS, parts=1)
        weights_at = sb("weights_at", SLOTS, I32, parts=1)
        biases_at = sb("biases_at", SLOTS, I32, parts=1)
        row_of = sb("row_of", SLOTS, I32, parts=1)
        padrows = sb("padrows", ROW)
        xh, xl = sb("xh", 2 * P, F32R), sb("xl", 2 * P, F32R)
        zb = sb("zb", PAIRS * D)
        xn = sb("xn", TB * D)
        xnT = sb("xnT", S)
        qk = sb("qk", 4 * S)
        v = sb("v", TB * D)
        scratch = sb("scratch", 5 * S + TB * QG * P)
        p1 = [scratch[:, i * S:(i + 1) * S] for i in range(3)]
        p2 = [scratch[:, (3 + i) * S:(4 + i) * S] for i in range(2)]
        dT = scratch[:, 5 * S:5 * S + TB * QG * P]
        at = [0]

        def lent(n):
            at[0] += n
            return scratch[:, at[0] - n:at[0]]

        xt, hs, hT, ys = lent(RING * ROW), lent(2 * F), lent(2 * F), lent(RING * D)
        cmp1, cmp2 = lent(E * NT)[0:1, :], lent(SLOTS * E)[0:1, :]
        eidf, offf, roff = (lent(SLOTS)[0:1, :] for _ in range(3))
        raw1, raw2 = scratch[:, 0:E * F], scratch[:, E * F:2 * E * F]
        mx, nb = sb("mx", 2 * TB), sb("nb", 2 * TB)
        l1, l2 = sb("l1", TB), sb("l2", TB)
        r1, r2, cc = sb("r1", TB), sb("r2", TB), sb("cc", TB)
        oT, ob = sb("oT", QG * P), sb("ob", QG * D)
        sq = sb("sq", QG * D)
        ss, so = sb("ss", TB), sb("so", TB)

        (w_loaded, small_loaded, masks_made, pool_step, dve_step, wT_ps, w_half, w1_sb, w2_sb, wr_ps,
         lam_in, lam_ps, lam_exp, ln_stats, ln_rstd, rows_ready, rows_copied, tgtT_ps, tgtT_sb, logits_ps, lg_read,
         gap_ready, gap_exp, cnt_ready, prefix_ps, slots_ready, table_ready, pads_sent,
         xT_ps, xh_ready, xl_ready, h_ps, h_sb, hT_ps, hT_sb, y_ps, y_sb,
         z_used, xn_ready, xnT_ps, xnT_sb, proj_ps, proj_act, proj_dve,
         v_ps, v_sb, s_ps, nb_ready, p_ready, diff_ready, dT_ps, dT_sb, oT_ps, oT_sb, o_ps, ob_ready, beta_added,
         ss_ready, so_ready, x_done, stored) = (sem(n) for n in (
            "w_loaded", "small_loaded", "masks_made", "pool_step", "dve_step", "wT_ps", "w_half",
            "w1_sb", "w2_sb", "wr_ps", "lam_in", "lam_ps", "lam_exp", "ln_stats", "ln_rstd", "rows_ready",
            "rows_copied", "tgtT_ps", "tgtT_sb", "logits_ps", "lg_read", "gap_ready", "gap_exp", "cnt_ready",
            "prefix_ps", "slots_ready", "table_ready", "pads_sent", "xT_ps", "xh_ready",
            "xl_ready", "h_ps", "h_sb", "hT_ps", "hT_sb", "y_ps", "y_sb", "z_used", "xn_ready",
            "xnT_ps", "xnT_sb", "proj_ps", "proj_act", "proj_dve", "v_ps", "v_sb",
            "s_ps", "nb_ready", "p_ready", "diff_ready", "dT_ps", "dT_sb", "oT_ps", "oT_sb", "o_ps",
            "ob_ready", "beta_added", "ss_ready", "so_ready", "x_done", "stored"))
        x_loaded = [sem(f"x_loaded{b}") for b in range(BATCHES)]
        xt_loaded = [sem(f"xt_loaded{r}") for r in range(RING)]
        rows_sent = [sem(f"rows_sent{par}") for par in range(2)]
        went_by = sem("went_by")
        z_loaded = [sem(f"z_loaded{h}") for h in range(2)]
        y_sent = [sem(f"y_sent{r}") for r in range(RING)]

        def cols(t, i, n):
            return t[:, i * n:(i + 1) * n] if isinstance(i, int) else t[:, bass.ds(i * n, n)]

        x_v = x_in.rearrange("b (p j) d -> b p (j d)", p=P)
        out_v = out.rearrange("b (p j) d -> b p (j d)", p=P)
        results_v = results.rearrange("(b p j) d -> b p (j d)", p=P, b=BATCHES)
        rowbuf_v = rowbuf[:, :].rearrange("p (a j k r) -> p a j k r", a=2, j=TB, k=2)
        mv = [mv2[:, i * 2 * TB:(i + 1) * 2 * TB].rearrange("p (j c) -> p j c", c=2) for i in range(2)]
        rs = [rs2[:, i * TB:(i + 1) * TB] for i in range(2)]
        bias_v = biases[:, :].rearrange("p (e c) -> p e c", e=E)
        dest_v = dest[:, :].rearrange("p (t k) -> p t k", k=2)
        slot_v = slot[:, :].rearrange("p (a j k) -> p a j k", a=2, k=2)
        xt_v = xt.rearrange("p (r c) -> p r c", r=RING)

        def by_expert(t):
            return t[:, :].rearrange("p (e t) -> p e t", e=E)

        def by_tile(t):
            return t[:, :].rearrange("p (e t) -> p t e", e=E)

        def over_experts(t):
            return t[:, :].unsqueeze(2).broadcast_to([P, TB, E])

        def over_tiles(t):
            return t[:, :].unsqueeze(2).broadcast_to([P, E, TB])

        def expert_offsets(eng, table, step, at, s, n):
            _, values = nc.values_load_multi_w_load_instructions(
                table[0:1, s:s + n] if isinstance(s, int) else table[0:1, bass.ds(s, n)], engines=[eng], min_val=0, max_val=(E - 1) * step,
                skip_runtime_bounds_check_because="VectorE clamps the table to the last expert")
            return {at + i: value for i, value in enumerate(values)}

        N_SMALL = 13
        GROUPS = TB // QG

        def wait_apart(eng, *waits):
            for sem, v in waits:
                eng.wait_ge(sem, v)
            eng.sem_inc(went_by, 1)

        block = ctx.enter_context(nc.Block())

        @block.sync
        def _(sp):
            for b in range(BATCHES):
                sp.dma_start(x[:, b * TB * D:(b + 1) * TB * D], x_v[b]).then_inc(x_loaded[b], 16)
            sp.dma_start(raw2.rearrange("d (e f) -> d e f", e=E), W2.rearrange("e d f -> d e f")).then_inc(w_loaded, 16)

            def experts(p):
                if p == 0:
                    sp.wait_ge(masks_made, 1)
                    sp.dma_start(rows[E * REGION:, :], padrows[:, :]).then_inc(pads_sent, 16)
                sp.wait_ge(table_ready, p + 1)
                for e in range(E):
                    at = sp.value_load(carry_i[0:1, e:e + 1], min_val=0, max_val=E * REGION)
                    sp.dma_start(rows[bass.ds(at, P), :], padrows[:, :]).then_inc(pads_sent, 16)
                sp.wait_ge(pads_sent, 16 * (1 + E * (p + 1)))
                for par in range(2):
                    sp.wait_ge(rows_sent[par], 16 * PAIRS * BATCHES // 2 * (p + 1))

                def load(lap, r, again):
                    s = lap * RING + r
                    at = sp.value_load(row_of[0:1, bass.ds(s, 1)], min_val=0, max_val=E * REGION)
                    if again:
                        wait_apart(sp, (xT_ps, SLOTS * p + s - RING + 1))
                        wait_apart(sp, (y_sent[r], 16 * (LAPS * p + lap)))
                    sp.dma_start(xt[:, r * ROW:(r + 1) * ROW], rows[bass.ds(at, P), :]).then_inc(xt_loaded[r], 16)

                for r in range(RING):
                    load(0, r, p > 0)
                with sp.Fori(1, LAPS) as lap:
                    for r in range(RING):
                        load(lap, r, True)
                for r in range(RING):
                    sp.wait_ge(y_sent[r], 16 * LAPS * (p + 1))

            def load_results(p, b):
                for h in range(2):
                    n = 2 * (BATCHES * p + b) + h
                    if n >= 2:
                        sp.wait_ge(z_used, n - 1)
                    c = slice(h * TB * D, (h + 1) * TB * D)
                    sp.dma_start(zb[:, c], results_v[b][:, c]).then_inc(z_loaded[h], 16)

            experts(0)
            for b in range(BATCHES):
                load_results(0, b)
            experts(1)
            for b in range(BATCHES):
                load_results(1, b)
                if b:
                    sp.wait_ge(x_done, b)
                    sp.dma_start(out_v[b - 1], x[:, (b - 1) * TB * D:b * TB * D]).then_inc(stored, 16)
            sp.wait_ge(x_done, BATCHES)
            sp.dma_start(out_v[BATCHES - 1], x[:, (BATCHES - 1) * TB * D:]).then_inc(stored, 16)
            sp.wait_ge(stored, 16 * BATCHES)

        @block.gpsimd
        def _(pool):
            steps = Steps(pool, pool_step)
            pool.memset(ident[:, :], 0.0)
            pool.memset(upper[:, :], 1.0)
            pool.memset(ones[:, :], 1.0)
            pool.memset(nhalf[:, :], -0.5)
            pool.memset(onesE[:, :], 1.0)
            pool.memset(padrows[:, :], 0.0)
            pool.memset(segm[:, :], 1.0)
            pool.iota(dest[:, :], [[2 * S, BATCHES], [2, TB], [1, 2]], base=0, channel_multiplier=2 * TB)
            pool.iota(base[:, :], [[REGION, E]], base=0, channel_multiplier=0, allow_small_or_imprecise_dtypes=True)
            pool.iota(first[:, :], [[-1, E], [0, TB]], base=E, channel_multiplier=0, allow_small_or_imprecise_dtypes=True)
            pool.iota(tile128[:, :], [[P, NT]], base=0, channel_multiplier=0, allow_small_or_imprecise_dtypes=True)
            steps.then(pool.iota(sidx[:, :], [[1, SLOTS]], base=0, channel_multiplier=0, allow_small_or_imprecise_dtypes=True))
            pool.affine_select(out=ident[:, :], in_=ident[:, :], compare_op=ALU.not_equal, fill=1.0, base=0,
                               pattern=[[-1, P]], channel_multiplier=1)
            pool.affine_select(out=upper[:, :], in_=upper[:, :], compare_op=ALU.is_gt, fill=0.0, base=0,
                               pattern=[[1, P]], channel_multiplier=-1)
            pool.iota(padrows[:, D:ROW].bitcast(I32), [[0, 1]], base=2 * N, channel_multiplier=1)
            steps.then(pool.affine_select(out=by_expert(segm), in_=by_expert(segm), compare_op=ALU.not_equal, fill=0.0, base=0,
                                          pattern=[[0, E], [1, TB]], channel_multiplier=0))
            pool.nop().then_inc(masks_made, 1)

            def rstd(n):
                wait_apart(pool, (ln_stats, n + 1))
                steps.then(pool.tensor_scalar(rs[n % 2], mv[n % 2][:, :, 1], EPS, 0.0, ALU.add, ALU.add))
                pool.tensor_tensor(rs[n % 2], rs[n % 2], nhalf[:, :], ALU.pow).then_inc(ln_rstd, 1)

            def add_beta(p):
                pool.wait_ge(rows_ready, BATCHES * (p + 1))
                for b in range(BATCHES):
                    xb = x[:, b * TB * D:(b + 1) * TB * D].rearrange("p (j d) -> p j d", j=TB)
                    pool.tensor_tensor(xb, xb, betab[:, :].unsqueeze(1).broadcast_to([P, TB, D]), ALU.add).then_inc(beta_added, 1)

            def scatter(p, b, par, tiles=range(TB)):
                if tiles[0] == 0:
                    wait_apart(pool, (slots_ready, BATCHES * p + b + 1), (rows_copied, BATCHES * p + b + 1))
                for j in tiles:
                    for k in range(2):
                        pool.indirect_dma_start(rows, bass.IndirectOffsetOnAxis(slot_v[:, par, j, k:k + 1], 0),
                                                rowbuf_v[:, par, j, k, :], None).then_inc(rows_sent[par], 16)

            def experts(p):
                def send(lap, r):
                    wait_apart(pool, (y_sb, SLOTS * p + lap * RING + r + 1))
                    pool.indirect_dma_start(results, bass.IndirectOffsetOnAxis(xt_v[:, r, D:ROW].bitcast(I32), 0),
                                            ys[:, r * D:(r + 1) * D], None, bounds_check=2 * N - 1,
                                            oob_is_err=False).then_inc(y_sent[r], 16)
                with pool.Fori(0, LAPS) as lap:
                    for r in range(RING):
                        send(lap, r)

            def value_scale(b, g):
                pool.wait_ge(ss_ready, GROUPS * b + g + 1)
                part = slice(g * QG, (g + 1) * QG)
                steps.then(pool.tensor_scalar(so[:, part], ss[:, part], OUT_GAIN / D, OUT_GAIN * EPS, ALU.mult, ALU.add))
                pool.tensor_tensor(so[:, part], so[:, part], nhalf[:, 0:QG], ALU.pow).then_inc(so_ready, 1)

            rstd(0)
            for b in range(BATCHES):
                if b + 1 < BATCHES:
                    rstd(b + 1)
                scatter(0, b, b % 2)
            add_beta(0)
            experts(0)
            n = BATCHES
            for _ in range(2):
                rstd(n)
                n += 1
            for b in range(BATCHES):
                if b:
                    rstd(n)
                    n += 1
                if b > 1:
                    scatter(1, b - 2, b % 2, range(TB // 2, TB))
                if b < BATCHES - 1:
                    rstd(n)
                    rstd(n + 1)
                    n += 2
                value_scale(b, 0)
                if b:
                    scatter(1, b - 1, (b - 1) % 2, range(TB // 2))
                value_scale(b, 1)
            rstd(n)
            assert n == 4 * BATCHES - 1
            scatter(1, BATCHES - 2, 0, range(TB // 2, TB))
            scatter(1, BATCHES - 1, 1)
            add_beta(1)
            experts(1)
            for b in range(BATCHES):
                rstd(4 * BATCHES + b)

        @block.scalar
        def _(act):
            act.dma_start(wr[:, :], Wr).then_inc(small_loaded, 16)
            act.dma_start(brb[:, :], br.partition_broadcast(P)).then_inc(small_loaded, 16)
            act.dma_start(qkw[:, 0:2 * D], w_q12).then_inc(small_loaded, 16)
            act.dma_start(qkw[:, 2 * D:4 * D], w_k12).then_inc(small_loaded, 16)
            act.dma_start(wv[:, :], w_v).then_inc(small_loaded, 16)
            for i, l in enumerate((lq1, lk1, lq2, lk2)):
                act.dma_start(lamv[:, i:i + 1], l.rearrange("(d a) -> d a", a=1)).then_inc(small_loaded, 16)
            act.dma_start(gammab[:, :], gamma.partition_broadcast(P)).then_inc(small_loaded, 16)
            act.dma_start(betab[:, :], beta.partition_broadcast(P)).then_inc(small_loaded, 16)
            act.dma_start(bias_v[:, :, FC:BIAS], b2.partition_broadcast(P)).then_inc(small_loaded, 16)
            act.dma_start(b1r, b1.rearrange("e (c f) -> (e c) f", f=P)).then_inc(small_loaded, 16)
            act.dma_start(raw1.rearrange("f (g d) -> f g d", d=D), W1.rearrange("e (c f) d -> f (e c) d", f=P)).then_inc(w_loaded, 16)

            def weights(experts):
                for g in experts:
                    act.wait_ge(wT_ps, 2 * g + 1)
                    act.activation(w1h[:, g * F:(g + 1) * F], bank(g % 2), ACT.Copy).then_inc(w_half, 1)
                    act.wait_ge(wT_ps, 2 * g + 2)
                    act.activation(w2T[:, g * F:(g + 1) * F], bank(2 + g % 2), ACT.Copy).then_inc(w2_sb, 1)

            def copy_rows(p, b, par):
                act.wait_ge(rows_ready, BATCHES * p + b + 1)
                rb = rowbuf_v[:, par, :, 0, 0:D]
                act.activation(rowbuf_v[:, par, :, 1, 0:D], rb, ACT.Copy)
                act.activation(cols(tgt, b, TB * D).rearrange("p (j d) -> p j d", j=TB), rb, ACT.Copy).then_inc(rows_copied, 1)

            def copy_tgtT(a, i):
                act.wait_ge(tgtT_ps, 2 * a + i + 1)
                act.activation(tgtT[:, i * 512:(i + 1) * 512], bank(7), ACT.Copy).then_inc(tgtT_sb, 1)

            def gap(a):
                act.wait_ge(gap_ready, a + 1)
                act.activation(ex[:, :], ex[:, :], ACT.Exp).then_inc(gap_exp, 1)

            def experts(p):
                def xh_part(s, u):
                    g = SLOTS * p + s
                    act.wait_ge(xT_ps, g + 1)
                    if p or not isinstance(s, int) or s >= 2:
                        act.wait_ge(h_ps, g - 1)
                    act.activation(xh[:, (u % 2) * P:(u % 2 + 1) * P], bank(u % 2, 0, P), ACT.Copy).then_inc(xh_ready, 1)

                def h_copy(s, u):
                    g, k = SLOTS * p + s, u % 2
                    act.wait_ge(h_ps, g + 1)
                    if p or not isinstance(s, int) or s >= 2:
                        act.wait_ge(hT_ps, g - 1)
                    act.activation(hs[:, k * F:(k + 1) * F], bank(2 + k), ACT.Copy).then_inc(h_sb, 1)

                xh_part(0, 0)
                for s in range(2):
                    xh_part(s + 1, s + 1)
                    h_copy(s, s)
                with act.Fori(1, SLOTS // 2 - 1) as i:
                    for u in range(2):
                        xh_part(i * 2 + u + 1, u + 1)
                        h_copy(i * 2 + u, u)
                xh_part(SLOTS - 1, 1)
                h_copy(SLOTS - 2, 0)
                h_copy(SLOTS - 1, 1)

            def copy_xnT(b, i):
                act.wait_ge(xnT_ps, 2 * b + i + 1)
                act.activation(xnT[:, i * 512:(i + 1) * 512], bank(7), ACT.Copy).then_inc(xnT_sb, 1)

            def copy_proj(b):
                for m in range(0, 8, 2):
                    act.wait_ge(proj_ps, 8 * b + m + 1)
                    act.activation(qk[:, m * 512:(m + 1) * 512], bank(m % 4), ACT.Copy).then_inc(proj_act, 1)

            def copy_v(b, i):
                act.wait_ge(v_ps, 2 * b + i + 1)
                act.activation(v[:, i * 512:(i + 1) * 512], bank(7), ACT.Copy).then_inc(v_sb, 1)

            def attention(b):
                def dT_copy(i):
                    act.wait_ge(dT_ps, TB * b + i + 1)
                    if i % QG == 0 and i:
                        act.wait_ge(oT_ps, GROUPS * b + i // QG)
                    act.activation(dT.rearrange("p (k q) -> p k q", k=TB)[:, :, (i % QG) * P:(i % QG + 1) * P],
                                   banks[:, 4 * 512:6 * 512].rearrange("p (k q) -> p k q", k=TB), ACT.Copy).then_inc(dT_sb, 1)

                def o_copy(g):
                    act.wait_ge(oT_ps, GROUPS * b + g + 1)
                    act.activation(oT[:, :], bank(6), ACT.Copy).then_inc(oT_sb, 1)

                def squares(b, g):
                    act.wait_ge(ob_ready, GROUPS * b + g + 1)
                    for q in range(QG):
                        i = g * QG + q
                        ins = act.activation(sq[:, q * D:(q + 1) * D], ob[:, q * D:(q + 1) * D], ACT.Square, accum_out=ss[:, i:i + 1])
                    ins.then_inc(ss_ready, 1)

                def probabilities(i):
                    for m, (pp, ll) in enumerate(((p1[i % 3], l1), (p2[i % 2], l2))):
                        act.wait_ge(nb_ready, 2 * (TB * b + i) + m + 1)
                        if m == 0 and TB * b + i >= 3:
                            act.wait_ge(dT_ps, TB * b + i - 2)
                        if m == 1 and TB * b + i >= 2:
                            act.wait_ge(diff_ready, TB * b + i - 1)
                        act.activation(pp, banks[:, 2 * m * 512:(2 * m + 2) * 512], ACT.Exp,
                                       bias=nb[:, 2 * i + m:2 * i + m + 1], scale=SCALE,
                                       accum_out=ll[:, i:i + 1]).then_inc(p_ready, 1)

                for i in range(TB):
                    probabilities(i)
                    if i == 0 and b:
                        squares(b - 1, 1)
                    if i >= 2:
                        dT_copy(i - 2)
                    if b and i == 3:
                        copy_rows(1, b - 1, (b - 1) % 2)
                    if b and i in (4, 5):
                        copy_tgtT(BATCHES + b - 1, i - 4)
                    if i == QG + 2:
                        o_copy(0)
                if b < BATCHES - 1:
                    for i in range(2):
                        copy_xnT(b + 1, i)
                dT_copy(TB - 2)
                if b < BATCHES - 1:
                    copy_proj(b + 1)
                squares(b, 0)
                if b:
                    gap(BATCHES + b - 1)
                dT_copy(TB - 1)
                if b < BATCHES - 1:
                    for i in range(2):
                        copy_v(b + 1, i)
                o_copy(1)

            def route(p, b, par):
                copy_rows(p, b, par)
                for i in range(2):
                    copy_tgtT(BATCHES * p + b, i)
                gap(BATCHES * p + b)

            for b in range(BATCHES):
                route(0, b, b % 2)
                if 0 < b < 3:
                    weights(range((b - 1) * E // 2, b * E // 2))
            act.wait_ge(lam_ps, 1)
            act.activation(lame[:, :], bank(5, 0, 2), ACT.Exp).then_inc(lam_exp, 1)
            experts(0)
            for i in range(2):
                copy_xnT(0, i)
            copy_proj(0)
            for i in range(2):
                copy_v(0, i)
            for b in range(BATCHES):
                attention(b)
            act.wait_ge(ob_ready, GROUPS * BATCHES)
            for q in range(QG):
                ins = act.activation(sq[:, q * D:(q + 1) * D], ob[:, q * D:(q + 1) * D], ACT.Square,
                                     accum_out=ss[:, QG + q:QG + q + 1])
            ins.then_inc(ss_ready, 1)
            route(1, BATCHES - 1, 1)
            experts(1)

        @block.tensor
        def _(pe):
            def three(o, ah, al, bh, bl):
                pe.matmul(o, ah, bh, start=True, stop=False)
                pe.matmul(o, ah, bl, start=False, stop=False)
                return pe.matmul(o, al, bh, start=False, stop=True)

            def small_weights():
                pe.wait_ge(masks_made, 1)
                pe.wait_ge(small_loaded, 16 * N_SMALL)
                pe.transpose(bank(4, 0, E), wr[:, :], ident[0:E, 0:E])
                pe.transpose(bank(4, E, E + E * FC), b1r, ident[0:E * FC, 0:E * FC]).then_inc(wr_ps, 1)

            def weights(experts):
                pe.wait_ge(w_loaded, 32)
                for g in experts:
                    if g >= 2:
                        pe.wait_ge(w1_sb, g - 1)
                        pe.wait_ge(w2_sb, g - 1)
                    for c in range(FC):
                        k = g * FC + c
                        ins = pe.transpose(bank(g % 2, c * P, (c + 1) * P), raw1[:, k * D:(k + 1) * D], ident[:, :])
                    ins.then_inc(wT_ps, 1)
                    for c in range(FC):
                        k = g * FC + c
                        ins = pe.transpose(bank(2 + g % 2, c * P, (c + 1) * P), raw2[:, k * P:(k + 1) * P], ident[:, :])
                    ins.then_inc(wT_ps, 1)

            def turn_rows(a, par, i):
                pe.wait_ge(rows_ready, a + 1)
                if i:
                    pe.wait_ge(tgtT_sb, 2 * a + 1)
                for j in range(4):
                    ins = pe.transpose(bank(7, j * P, (j + 1) * P), rowbuf_v[:, par, 4 * i + j, 0, 0:D], ident[:, :])
                ins.then_inc(tgtT_ps, 1)

            def logits(a):
                pe.wait_ge(tgtT_sb, 2 * a + 2)
                lo = bank(7, 0, G).rearrange("p (e t) -> p e t", e=E)
                for j in range(TB):
                    ins = pe.matmul(lo[:, :, j], tgtT[:, j * P:(j + 1) * P], wrT[:, :], start=True, stop=True)
                ins.then_inc(logits_ps, 1)

            def prefix(a):
                pe.wait_ge(cnt_ready, a + 1)
                pe.matmul(bank(7, 0, G), upper[:, :], cnt[:, :], start=True, stop=True)
                pe.matmul(bank(7, G, 2 * G), ones[:, :], cnt[:, :], start=True, stop=True).then_inc(prefix_ps, 1)

            def route(a, par):
                for i in range(2):
                    turn_rows(a, par, i)
                logits(a)
                prefix(a)

            def experts(p):
                def later(s, n):
                    return p > 0 or not isinstance(s, int) or s >= n

                def turn_x(s, u):
                    g, r = SLOTS * p + s, u % RING
                    lap = s // RING if isinstance(s, int) else s_lap[0] + u // RING
                    pe.wait_ge(xt_loaded[r], 16 * (LAPS * p + lap + 1))
                    if later(s, 2):
                        pe.wait_ge(xl_ready, g - 1)
                    pe.transpose(bank(u % 2, 0, P), xt_v[:, r, 0:D], ident[:, :]).then_inc(xT_ps, 1)

                def first(s, u):
                    g, k = SLOTS * p + s, u % 2
                    pe.wait_ge(xl_ready, g + 1)
                    if later(s, 2):
                        pe.wait_ge(h_sb, g - 1)
                    three(bank(2 + k), xh[:, k * P:(k + 1) * P], xl[:, k * P:(k + 1) * P],
                          w1h[:, bass.ds(w_at[u], F)], w1l[:, bass.ds(w_at[u], F)]).then_inc(h_ps, 1)

                def turn_h(s, u):
                    g, k = SLOTS * p + s, u % 2
                    pe.wait_ge(h_sb, g + 1)
                    if later(s, 2):
                        pe.wait_ge(hT_sb, g - 1)
                    for c in range(FC):
                        ins = pe.transpose(bank(4 + k, c * P, (c + 1) * P), hs[:, k * F + c * P:k * F + (c + 1) * P], ident[:, :])
                    ins.then_inc(hT_ps, 1)

                def second(s, u):
                    g, k = SLOTS * p + s, u % 2
                    pe.wait_ge(hT_sb, g + 1)
                    if later(s, 2):
                        pe.wait_ge(y_sb, g - 1)
                    for c in range(FC):
                        ins = pe.matmul(bank(6 + k, 0, D), hT[:, k * F + c * P:k * F + (c + 1) * P],
                                        w2T[:, c * D:][:, bass.ds(w_at[u], D)], start=(c == 0), stop=(c == FC - 1))
                    ins.then_inc(y_ps, 1)

                def step(s, u):
                    known = isinstance(s, int)
                    if not known or s + 2 < SLOTS:
                        turn_x(s + 2, u + 2)
                    if not known or 0 <= s + 1 < SLOTS:
                        first(s + 1, u + 1)
                    if not known or 0 <= s < SLOTS:
                        turn_h(s, u)
                    if not known or s >= 1:
                        second(s - 1, u - 1)

                s_lap, w_at = [0], {}
                w_at.update(expert_offsets(PE, weights_at, F, 0, 0, 4))
                for s in range(-2, 3):
                    step(s, s)
                with pe.Fori(0, LAPS - 1) as lap:
                    s_lap[0] = lap
                    w_at.update(expert_offsets(PE, weights_at, F, 0, lap * RING, RING + 4))
                    for u in range(3, RING + 3):
                        step(lap * RING + u, u)
                tail = (LAPS - 1) * RING
                w_at.update(expert_offsets(PE, weights_at, F, tail, tail, RING))
                for s in range(tail + 3, SLOTS + 1):
                    step(s, s)

            def turn_xn(b, i):
                pe.wait_ge(xn_ready, b + 1)
                if i:
                    pe.wait_ge(xnT_sb, 2 * b + 1)
                for j in range(4):
                    t = 4 * i + j
                    ins = pe.transpose(bank(7, j * P, (j + 1) * P), xn[:, t * D:(t + 1) * D], ident[:, :])
                ins.then_inc(xnT_ps, 1)

            def project(b):
                pe.wait_ge(xnT_sb, 2 * b + 2)
                for m in range(8):
                    h = slice((m % 2) * 512, (m % 2 + 1) * 512)
                    if m >= 4:
                        pe.wait_ge((proj_act, proj_dve)[m % 2], 4 * b + (m - 4) // 2 + 1)
                    elif b:
                        pe.wait_ge(p_ready, 2 * TB * b - 1 + m // 2)
                    pe.matmul(bank(m % 4), qkw[:, (m // 2) * D:(m // 2 + 1) * D], xnT[:, h], start=True, stop=True).then_inc(proj_ps, 1)

            def project_v(b, i):
                if i:
                    pe.wait_ge(v_sb, 2 * b + 1)
                for j in range(4):
                    t = slice((4 * i + j) * P, (4 * i + j + 1) * P)
                    ins = pe.matmul(bank(7, j * P, (j + 1) * P), xnT[:, t], wv[:, :], start=True, stop=True)
                ins.then_inc(v_ps, 1)

            def attention(b):
                def scores(i):
                    for m in range(2):
                        if i:
                            pe.wait_ge(p_ready, 2 * (TB * b + i) + m - 1)
                        for h in range(2):
                            k = slice((2 + m) * S + h * 512, (2 + m) * S + (h + 1) * 512)
                            ins = pe.matmul(bank(2 * m + h), qk[:, m * S + i * P:m * S + (i + 1) * P], qk[:, k], start=True, stop=True)
                        ins.then_inc(s_ps, 1)

                def turn(i):
                    pe.wait_ge(diff_ready, TB * b + i + 1)
                    if TB * b + i:
                        pe.wait_ge(dT_sb, TB * b + i)
                    for k in range(TB):
                        ins = pe.transpose(bank(4 + k // 4, (k % 4) * P, (k % 4 + 1) * P), p1[i % 3][:, k * P:(k + 1) * P], ident[:, :])
                    ins.then_inc(dT_ps, 1)

                def values(g):
                    pe.wait_ge(dT_sb, TB * b + (g + 1) * QG)
                    if GROUPS * b + g:
                        pe.wait_ge(ob_ready, GROUPS * b + g)
                    for k in range(TB):
                        ins = pe.matmul(bank(6), v[:, k * D:(k + 1) * D], dT[:, k * QG * P:(k + 1) * QG * P],
                                        start=(k == 0), stop=(k == TB - 1))
                    ins.then_inc(oT_ps, 1)

                def turn_back(g):
                    pe.wait_ge(oT_sb, GROUPS * b + g + 1)
                    for q in range(QG):
                        ins = pe.transpose(bank(6, q * P, (q + 1) * P), oT[:, q * P:(q + 1) * P], ident[:, :])
                    ins.then_inc(o_ps, 1)

                a = BATCHES + b - 1
                pe.wait_ge(proj_act, 4 * b + 4)
                pe.wait_ge(proj_dve, 4 * b + 4)
                for i in range(TB):
                    scores(i)
                    if i == QG + 2:
                        values(0)
                    if i >= 2:
                        turn(i - 2)
                    if b and i in (3, 4):
                        turn_rows(a, (b - 1) % 2, i - 3)
                    if b and i == 5:
                        logits(a)
                turn_back(0)
                if b:
                    pe.wait_ge(lg_read, a + 1)
                if b < BATCHES - 1:
                    for i in range(2):
                        turn_xn(b + 1, i)
                turn(TB - 2)
                if b < BATCHES - 1:
                    project(b + 1)
                if b:
                    prefix(a)
                turn(TB - 1)
                values(1)
                if b:
                    pe.wait_ge(slots_ready, a + 1)
                if b < BATCHES - 1:
                    for i in range(2):
                        project_v(b + 1, i)
                turn_back(1)

            small_weights()
            for b in range(BATCHES):
                route(b, b % 2)
                if 0 < b < 3:
                    weights(range((b - 1) * E // 2, b * E // 2))
            pe.wait_ge(lam_in, 1)
            pe.matmul(bank(5, 0, 2), ones[:, :], lamp[:, :], start=True, stop=True).then_inc(lam_ps, 1)
            pe.wait_ge(w1_sb, E)
            pe.wait_ge(w2_sb, E)
            pe.wait_ge(lam_exp, 1)
            pe.wait_ge(table_ready, 1)
            experts(0)
            for i in range(2):
                turn_xn(0, i)
            project(0)
            for i in range(2):
                project_v(0, i)
            for b in range(BATCHES):
                attention(b)
            route(2 * BATCHES - 1, 1)
            pe.wait_ge(table_ready, 2)
            experts(1)

        @block.vector
        def _(dve):
            steps = Steps(dve, dve_step)

            def small_weights():
                dve.wait_ge(wr_ps, 1)
                dve.tensor_copy(wrT[:, :], bank(4, 0, E))
                dve.tensor_copy(bias_v[:, :, 0:FC], bank(4, E, E + E * FC).rearrange("p (e c) -> p e c", e=E))
                dve.tensor_copy(by_expert(brt), over_tiles(brb))
                dve.tensor_copy(carry[:, :], base[:, :])
                dve.tensor_scalar(gammab[:, :], gammab[:, :], 0.5, None, ALU.mult)
                dve.tensor_scalar(betab[:, :], betab[:, :], 0.5, None, ALU.mult)
                dve.tensor_tensor(lamp[:, 0:1], lamv[:, 0:1], lamv[:, 1:2], ALU.mult)
                dve.tensor_tensor(lamp[:, 1:2], lamv[:, 2:3], lamv[:, 3:4], ALU.mult).then_inc(lam_in, 1)

            def weights(experts):
                for g in experts:
                    dve.wait_ge(w_half, g + 1)
                    dve.tensor_tensor(w1l[:, g * F:(g + 1) * F], bank(g % 2), w1h[:, g * F:(g + 1) * F].bitcast(F32),
                                      ALU.subtract).then_inc(w1_sb, 1)

            def minus_lambda():
                dve.wait_ge(lam_exp, 1)
                steps.then(dve.tensor_tensor(nlam[:, :], lame[:, 1:2], lame[:, 0:1], ALU.subtract))
                steps.then(dve.tensor_scalar(nlam[:, :], nlam[:, :], -LAMBDA_INIT, None, ALU.add))

            def linked(ins):
                ins.then_inc(dve_step, 1)
                steps.n += 1
                wait_apart(dve, (dve_step, steps.start + steps.n))

            def tile_stats(st, src, tiles=range(TB)):
                for j in tiles:
                    ins = dve.bn_stats(st[:, j * 6:(j + 1) * 6], src(j))
                return ins

            def batch_stats(st, n):
                for j in range(TB):
                    ins = dve.bn_aggr(mv[n % 2][:, j, :], st[:, j * 6:(j + 1) * 6])
                ins.then_inc(ln_stats, 1)

            def normalise(dst, src, n):
                dve.wait_ge(ln_rstd, n + 1)
                for j in range(TB):
                    ins = dve.tensor_scalar(dst(j), src(j), mv[n % 2][:, j, 0:1], rs[n % 2][:, j:j + 1], ALU.subtract, ALU.mult)
                return ins

            def x_tile(b):
                return lambda j: x[:, (b * TB + j) * D:(b * TB + j + 1) * D]

            def xn_tile(j):
                return xn[:, j * D:(j + 1) * D]

            def x_stats(b, n):
                if n:
                    dve.wait_ge(ln_stats, n)
                linked(tile_stats(st_x, x_tile(b)))
                batch_stats(st_x, n)

            def make_rows(p, b, n):
                par, sent = b % 2, BATCHES // 2 * p + b // 2
                if sent:
                    dve.wait_ge(rows_sent[par], 16 * PAIRS * sent)
                normalise(lambda j: rowbuf_v[:, par, j, 0, 0:D], x_tile(b), n)
                dve.tensor_copy(rowbuf_v[:, par, :, :, D].bitcast(I32), dest_v[:, b * TB:(b + 1) * TB, :]).then_inc(rows_ready, 1)

            def read_logits(a):
                dve.wait_ge(logits_ps, a + 1)
                dve.tensor_tensor(lg[:, :], bank(7, 0, G), brt[:, :], ALU.add).then_inc(lg_read, 1)

            def choose(a):
                dve.wait_ge(lg_read, a + 1)
                for m, oh in ((m1, oh1), (m2, oh2)):
                    steps.then(dve.tensor_reduce(m[:, :], by_tile(lg), AX_X, ALU.max))
                    steps.then(dve.tensor_tensor(by_tile(eq), by_tile(lg), over_experts(m), ALU.is_equal))
                    steps.then(dve.tensor_tensor(eq[:, :], eq[:, :], first[:, :], ALU.mult))
                    steps.then(dve.tensor_reduce(kk[:, :], by_tile(eq), AX_X, ALU.max))
                    steps.then(dve.tensor_tensor(by_tile(oh), by_tile(eq), over_experts(kk), ALU.is_equal))
                    if oh is oh1:
                        steps.then(dve.scalar_tensor_tensor(lg[:, :], oh1[:, :], -3.0e38, lg[:, :], ALU.mult, ALU.add))
                dve.tensor_tensor(cnt[:, :], oh1[:, :], oh2[:, :], ALU.add).then_inc(cnt_ready, 1)
                dve.tensor_tensor(ex[:, :], m2[:, :], m1[:, :], ALU.subtract).then_inc(gap_ready, 1)

            def place(a, b):
                par = b % 2
                dve.wait_ge(gap_exp, a + 1)
                steps.then(dve.tensor_scalar(den[:, :], ex[:, :], 1.0, None, ALU.add))
                w = wts[:, b * 2 * TB:(b + 1) * 2 * TB].rearrange("p (t k) -> p t k", k=2)
                steps.then(dve.reciprocal(den[:, :], den[:, :]))
                dve.tensor_copy(w[:, :, 0], den[:, :])
                dve.tensor_tensor(w[:, :, 1], ex[:, :], den[:, :], ALU.mult)
                dve.wait_ge(prefix_ps, a + 1)
                steps.then(dve.tensor_tensor_scan(run[:, :], segm[:, :], bank(7, G, 2 * G), 0.0, ALU.mult, ALU.add))
                steps.then(dve.tensor_tensor(pos[:, :], run[:, :], bank(7, G, 2 * G), ALU.subtract))
                steps.then(dve.tensor_tensor(pos[:, :], pos[:, :], bank(7, 0, G), ALU.add))
                steps.then(dve.tensor_tensor(by_expert(pos), by_expert(pos), over_tiles(carry), ALU.add))
                steps.then(dve.tensor_tensor(carry[:, :], carry[:, :], by_expert(run)[:, :, TB - 1], ALU.add))
                sv = slotf[:, :].rearrange("p (t k) -> p t k", k=2)
                for k, oh in enumerate((oh1, oh2)):
                    steps.then(dve.tensor_tensor(eq[:, :], oh[:, :], pos[:, :], ALU.mult))
                    steps.then(dve.tensor_reduce(sv[:, :, k], by_tile(eq), AX_X, ALU.add))
                dve.tensor_copy(slot[:, par * 2 * TB:(par + 1) * 2 * TB], slotf[:, :]).then_inc(slots_ready, 1)

            def route(p, b, n):
                make_rows(p, b, n)
                read_logits(BATCHES * p + b)
                choose(BATCHES * p + b)
                place(BATCHES * p + b, b)

            def table():
                dve.tensor_copy(carry_i[:, :], carry[:, :])
                steps.then(dve.tensor_tensor(carry[:, :], carry[:, :], base[:, :], ALU.subtract))
                c1 = cmp1[:, :].rearrange("p (e t) -> p e t", e=E)
                steps.then(dve.tensor_tensor(c1, carry[0:1, :].unsqueeze(2).broadcast_to([1, E, NT]),
                                             tile128[:, :].unsqueeze(1).broadcast_to([1, E, NT]), ALU.is_gt))
                steps.then(dve.tensor_reduce(ntile[:, :], c1, AX_X, ALU.add))
                steps.then(dve.tensor_tensor_scan(tend[:, :], onesE[:, :], ntile[:, :], 0.0, ALU.mult, ALU.add))
                c2 = cmp2[:, :].rearrange("p (s e) -> p s e", e=E)
                steps.then(dve.tensor_tensor(c2, sidx[:, :].unsqueeze(2).broadcast_to([1, SLOTS, E]),
                                             tend[:, :].unsqueeze(1).broadcast_to([1, SLOTS, E]), ALU.is_ge))
                steps.then(dve.tensor_reduce(eidf[:, :], c2, AX_X, ALU.add))
                steps.then(dve.tensor_tensor(c2, c2, ntile[:, :].unsqueeze(1).broadcast_to([1, SLOTS, E]), ALU.mult))
                steps.then(dve.tensor_reduce(offf[:, :], c2, AX_X, ALU.add))
                steps.then(dve.tensor_tensor(offf[:, :], sidx[:, :], offf[:, :], ALU.subtract))
                steps.then(dve.tensor_scalar(offf[:, :], offf[:, :], float(P), None, ALU.mult))
                steps.then(dve.scalar_tensor_tensor(roff[:, :], eidf[:, :], float(REGION), offf[:, :], ALU.mult, ALU.add))
                dve.tensor_scalar(row_of[:, :], roff[:, :], float(E * REGION), None, ALU.min)
                dve.tensor_scalar(weights_at[:, :], eidf[:, :], float(E - 1), float(F), ALU.min, ALU.mult)
                steps.then(dve.tensor_scalar(biases_at[:, :], eidf[:, :], float(E - 1), float(BIAS), ALU.min, ALU.mult))
                dve.tensor_copy(carry[:, :], base[:, :]).then_inc(table_ready, 1)

            def experts(p):
                def later(s, n):
                    return p > 0 or not isinstance(s, int) or s >= n

                def x_rest(s, u):
                    g, k = SLOTS * p + s, u % 2
                    dve.wait_ge(xh_ready, g + 1)
                    dve.tensor_tensor(xl[:, k * P:(k + 1) * P], bank(k, 0, P), xh[:, k * P:(k + 1) * P].bitcast(F32),
                                      ALU.subtract).then_inc(xl_ready, 1)

                def relu(s, u):
                    g, k = SLOTS * p + s, u % 2
                    dve.wait_ge(hT_ps, g + 1)
                    if later(s, 2):
                        dve.wait_ge(y_ps, g - 1)
                    for c in range(FC):
                        ins = dve.tensor_scalar(hT[:, k * F + c * P:k * F + (c + 1) * P], bank(4 + k, c * P, (c + 1) * P),
                                                biases[:, c:][:, bass.ds(b_at[u], 1)], 0.0, ALU.add, ALU.max)
                    ins.then_inc(hT_sb, 1)

                def add_b2(s, u):
                    g, k, r = SLOTS * p + s, u % 2, u % RING
                    lap = s // RING if isinstance(s, int) else s_lap[0] + u // RING
                    dve.wait_ge(y_ps, g + 1)
                    if later(s, RING):
                        dve.wait_ge(y_sent[r], 16 * (LAPS * p + lap))
                    dve.tensor_tensor(ys[:, r * D:(r + 1) * D], bank(6 + k, 0, D), biases[:, FC:][:, bass.ds(b_at[u], D)], ALU.add).then_inc(y_sb, 1)

                def step(s, u):
                    known = isinstance(s, int)
                    if not known or s + 2 < SLOTS:
                        x_rest(s + 2, u + 2)
                    if not known or 0 <= s < SLOTS:
                        relu(s, u)
                    if not known or s >= 1:
                        add_b2(s - 1, u - 1)

                s_lap, b_at = [0], {}
                b_at.update(expert_offsets(DVE, biases_at, BIAS, 0, 0, RING + 4))
                for s in range(-2, RING + 3):
                    step(s, s)
                with dve.Fori(1, LAPS - 1) as lap:
                    s_lap[0] = lap
                    b_at.update(expert_offsets(DVE, biases_at, BIAS, 0, lap * RING, RING + 4))
                    for u in range(3, RING + 3):
                        step(lap * RING + u, u)
                tail = (LAPS - 1) * RING
                b_at.update(expert_offsets(DVE, biases_at, BIAS, tail, tail, RING))
                for s in range(tail + 3, SLOTS + 1):
                    step(s, s)

            def merge_tiles(p, b, tiles):
                h = tiles[0] * 2 // TB
                dve.wait_ge(z_loaded[h], 16 * (BATCHES * p + b + 1))

                def w(j, k):
                    c = (b * TB + j) * 2 + k
                    return wts[:, c:c + 1]

                for j in tiles:
                    c = (b * TB + j) * D
                    ins = dve.scalar_tensor_tensor(xn_tile(j), zb[:, 2 * j * D:(2 * j + 1) * D], w(j, 0), tgt[:, c:c + D], ALU.mult, ALU.add)
                steps.then(ins)
                for j in tiles:
                    ins = dve.scalar_tensor_tensor(xn_tile(j), zb[:, (2 * j + 1) * D:(2 * j + 2) * D], w(j, 1), xn_tile(j), ALU.mult, ALU.add)
                if (tiles[-1] + 1) * 2 % TB == 0:
                    ins.then_inc(z_used, 1)
                    dve.wait_ge(z_used, 2 * (BATCHES * p + b) + h + 1)
                else:
                    steps.then(ins)
                return tile_stats(st_r, xn_tile, tiles)

            def merge_center(n):
                dve.wait_ge(ln_stats, n + 1)
                for j in range(TB):
                    ins = dve.scalar_tensor_tensor(xn_tile(j), xn_tile(j), mv[n % 2][:, j, 0:1], gammab[:, :], ALU.subtract, ALU.mult)
                steps.then(ins)

            def merge_add(p, b, n):
                dve.wait_ge(ln_rstd, n + 1)
                dve.wait_ge(beta_added, BATCHES * p + b + 1)
                for j in range(TB):
                    xj = x_tile(b)(j)
                    ins = dve.scalar_tensor_tensor(xj, xn_tile(j), rs[n % 2][:, j:j + 1], xj, ALU.mult, ALU.add)
                if p:
                    ins.then_inc(x_done, 1)
                    dve.wait_ge(x_done, b + 1)
                else:
                    steps.then(ins)

            def merge(p, b, n):
                for h in range(2):
                    ins = merge_tiles(p, b, range(h * TB // 2, (h + 1) * TB // 2))
                linked(ins)
                batch_stats(st_r, n)
                merge_center(n)
                merge_add(p, b, n)

            def make_xn(b, n):
                normalise(xn_tile, x_tile(b), n).then_inc(xn_ready, 1)

            def copy_proj(b, ms):
                for m in ms:
                    dve.wait_ge(proj_ps, 8 * b + m + 1)
                    dve.tensor_copy(qk[:, m * 512:(m + 1) * 512], bank(m % 4)).then_inc(proj_dve, 1)

            def scale_values(b, g):
                dve.wait_ge(o_ps, GROUPS * b + g + 1)
                for q in range(QG):
                    i = g * QG + q
                    ins = dve.tensor_scalar(ob[:, q * D:(q + 1) * D], bank(6, q * P, (q + 1) * P), r1[:, i:i + 1], None, ALU.mult)
                ins.then_inc(ob_ready, 1)

            def add_values(b, g):
                dve.wait_ge(so_ready, GROUPS * b + g + 1)
                for q in range(QG):
                    i = g * QG + q
                    xi = x_tile(b)(i)
                    ins = dve.scalar_tensor_tensor(xi, ob[:, q * D:(q + 1) * D], so[:, i:i + 1], xi, ALU.mult, ALU.add)
                steps.then(ins)

            def attention(b, n):
                def maxima(i):
                    for m in range(2):
                        c = slice(2 * i + m, 2 * i + m + 1)
                        dve.wait_ge(s_ps, 2 * (TB * b + i) + m + 1)
                        steps.then(dve.tensor_reduce(mx[:, c], banks[:, 2 * m * 512:(2 * m + 2) * 512], AX_X, ALU.max))
                        dve.tensor_scalar(nb[:, c], mx[:, c], -SCALE, None, ALU.mult).then_inc(nb_ready, 1)

                def difference(i):
                    c = slice(i, i + 1)
                    dve.wait_ge(p_ready, 2 * (TB * b + i) + 2)
                    dve.reciprocal(r1[:, c], l1[:, c])
                    steps.then(dve.reciprocal(r2[:, c], l2[:, c]))
                    steps.then(dve.tensor_scalar(cc[:, c], l1[:, c], r2[:, c], nlam[:, 0:1], ALU.mult, ALU.mult))
                    dve.scalar_tensor_tensor(p1[i % 3], p2[i % 2], cc[:, c], p1[i % 3], ALU.mult, ALU.add).then_inc(diff_ready, 1)

                last, after = b > 0, b < BATCHES - 1
                a = BATCHES + b - 1
                for i in range(TB):
                    maxima(i)
                    if i:
                        difference(i - 1)
                    if last and i == 0:
                        scale_values(b - 1, 1)
                    if last and i == 1:
                        add_values(b - 1, 1)
                    if last and i == 2:
                        x_stats(b - 1, n)
                    if last and i == 3:
                        make_rows(1, b - 1, n)
                        n += 1
                    if after and i < 4:
                        ins = merge_tiles(0, b + 1, range(2 * i, 2 * i + 2))
                    if after and i == 3:
                        linked(ins)
                        batch_stats(st_r, n)
                    if after and i == 4:
                        merge_center(n)
                        merge_add(0, b + 1, n)
                        n += 1
                    if after and i == 5:
                        x_stats(b + 1, n)
                    if after and i == 6:
                        make_xn(b + 1, n)
                        n += 1
                    if last and i == 7:
                        read_logits(a)
                scale_values(b, 0)
                if after:
                    copy_proj(b + 1, (1, 3))
                if last:
                    choose(a)
                if after:
                    copy_proj(b + 1, (5, 7))
                difference(TB - 1)
                add_values(b, 0)
                if last:
                    place(a, b - 1)
                return n

            for b in range(2):
                dve.wait_ge(x_loaded[b], 16)
                x_stats(b, b)
            small_weights()
            for b in range(BATCHES):
                route(0, b, b)
                if b < 2:
                    dve.wait_ge(x_loaded[b + 2], 16)
                    x_stats(b + 2, b + 2)
                if 0 < b < 3:
                    weights(range((b - 1) * E // 2, b * E // 2))
            minus_lambda()
            table()
            experts(0)
            n = BATCHES
            merge(0, 0, n)
            x_stats(0, n + 1)
            make_xn(0, n + 1)
            copy_proj(0, (1, 3, 5, 7))
            n += 2
            for b in range(BATCHES):
                n = attention(b, n)
            scale_values(BATCHES - 1, 1)
            add_values(BATCHES - 1, 1)
            x_stats(BATCHES - 1, n)
            route(1, BATCHES - 1, n)
            table()
            experts(1)
            for b in range(BATCHES):
                merge(1, b, n + 1 + b)


_INS = ['L0_attn_x', 'L0_attn_w_q12', 'L0_attn_w_k12', 'L0_attn_w_v', 'L0_attn_lambda_q1', 'L0_attn_lambda_k1',
        'L0_attn_lambda_q2', 'L0_attn_lambda_k2', 'L0_ffn_Wr', 'L0_ffn_br', 'L0_ffn_W1', 'L0_ffn_b1', 'L0_ffn_W2',
        'L0_ffn_b2', 'L0_ffn_gamma', 'L0_ffn_beta']
_OUTS = [((4, 1024, 128), 'float32')]


def kernel(**inputs):
    import numpy as _np
    import concourse.bacc as _bacc
    from concourse import mybir as _mybir
    from concourse.bass_utils import run_bass_kernel_spmd as _run

    nc = _bacc.Bacc("TRN2", target_bir_lowering=False, num_devices=1)
    arrays, args = {}, []
    for name in _INS:
        a = _np.ascontiguousarray(inputs[name])
        arrays[f"in_{name}_dram"] = a
        args.append(nc.dram_tensor(f"in_{name}_dram", a.shape, _mybir.dt.from_np(a.dtype), kind="ExternalInput").ap())
    for i, (shape, dtype) in enumerate(_OUTS):
        dt = _mybir.dt.from_np(_np.dtype(dtype))
        args.append(nc.dram_tensor(f"out_{i}_dram", shape, dt, kind="ExternalOutput").ap())
    macaron_kernel(nc, *args)
    r = _run(nc, [arrays], core_ids=[0])
    return r.results[0]["out_0_dram"]
```

```python
import concourse.bass as bass
from concourse import mybir
from contextlib import ExitStack

F32 = mybir.dt.float32
F32R = mybir.dt.float32r
I32 = mybir.dt.int32
ALU = mybir.AluOpType
ACT = mybir.ActivationFunctionType
AX_X = mybir.AxisListType.X
PE, DVE = mybir.EngineType.PE, mybir.EngineType.DVE

P = 128


class Steps:

    def __init__(self, eng, sem):
        self.eng, self.sem, self.start, self.n = eng, sem, 0, 0

    def begin(self, start):
        self.start, self.n = start, 0

    def then(self, ins):
        ins.then_inc(self.sem, 1)
        self.n += 1
        self.eng.wait_ge(self.sem, self.start + self.n)


def macaron_kernel(nc, x_in, w_q12, w_k12, w_v, lq1, lk1, lq2, lk2, Wr, br, W1, b1, W2, b2, gamma, beta, out):
    BATCHES, S, D = x_in.shape
    E, F, _ = W1.shape
    TB = S // P
    NT = BATCHES * TB
    N = BATCHES * S
    FC = F // P
    PAIRS = 2 * TB
    REGION = N + P
    ROW = D + 1
    SLOTS = -(-(2 * N // P + E - 1) // 8) * 8
    RING = 8
    LAPS = SLOTS // RING
    EPS = 1e-5
    SCALE = float(D) ** -0.25
    LAMBDA_INIT = 0.8
    OUT_GAIN = (1.0 - LAMBDA_INIT) ** -2
    QG = 4
    assert D == P and S == TB * P and F % P == 0 and SLOTS % RING == 0 and TB % QG == 0
    assert SLOTS - 2 * N // P <= 8

    rows = nc.dram_tensor("rows", [E * REGION + P, ROW], F32).ap()
    results = nc.dram_tensor("results", [2 * N, D], F32).ap()

    ctx = ExitStack()
    with ctx:
        def sb(name, cols, dt=F32, parts=P):
            return ctx.enter_context(nc.sbuf_tensor(name, [parts, cols], dt))

        def sem(name):
            return ctx.enter_context(nc.semaphore(name))

        banks = ctx.enter_context(nc.psum_tensor("banks", [P, 8 * 512], F32))

        def bank(i, a=0, b=512):
            return banks[:, i * 512 + a:i * 512 + b]

        x = sb("x", NT * D)
        tgt = sb("tgt", NT * D)
        w1h, w1l = sb("w1h", E * F, F32R), sb("w1l", E * F, F32R)
        w2T = sb("w2T", E * FC * D)
        BIAS = FC + D
        biases = sb("biases", E * BIAS)
        gammab, betab = sb("gammab", D), sb("betab", D)
        brb = sb("brb", E)
        brt = sb("brt", E * TB)
        wrT = sb("wrT", E)
        wr = tgt[0:E, 0:D]
        b1r = tgt[0:E * FC, 6 * D:7 * D]
        Mh, Ml = sb("Mh", 2 * D, F32R), sb("Ml", 2 * D, F32R)
        wv = sb("wv", D)
        ident, ones, upper = sb("ident", P), sb("ones", P), sb("upper", P)
        lamv, lamp, lame, nlam = sb("lamv", 4), sb("lamp", 2), sb("lame", 2), sb("nlam", 1)
        nhalf = sb("nhalf", TB)
        st_x, st_r = sb("st_x", TB * 6), sb("st_r", TB * 6)
        LN = 4
        mvs, rss, nms = sb("mv", LN * TB * 2), sb("rs", LN * TB), sb("nm", LN * TB)
        rowbuf = sb("rowbuf", 2 * TB * 2 * ROW)
        dest = sb("dest", NT * 2, I32)
        G = E * TB
        lg, eq, oh1, oh2, cnt, pos = (sb(n, G) for n in ("lg", "eq", "oh1", "oh2", "cnt", "pos"))
        run = lg
        first, segm = sb("first", G), sb("segm", G)
        m1, m2, kk, ex, den = (sb(n, TB) for n in ("m1", "m2", "kk", "ex", "den"))
        wts = sb("wts", NT * 2)
        slotf, slot = sb("slotf", 2 * TB), sb("slot", 2 * 2 * TB, I32)
        carry, base = sb("carry", E), sb("base", E)
        carry_i = sb("carry_i", E, I32)
        tile128 = sb("tile128", NT, parts=1)
        ntile, tend, onesE = sb("ntile", E, parts=1), sb("tend", E, parts=1), sb("onesE", E, parts=1)
        sidx = sb("sidx", SLOTS, parts=1)
        weights_at = sb("weights_at", SLOTS, I32, parts=1)
        biases_at = sb("biases_at", SLOTS, I32, parts=1)
        row_of = sb("row_of", SLOTS, I32, parts=1)
        padrows = sb("padrows", ROW)
        xn = [sb(f"xn{i}", TB * D) for i in range(2)]
        sum_r = sb("sum_r", TB * D)
        xnTh, xnTl = sb("xnTh", S, F32R), sb("xnTl", S, F32R)
        xh, xl = xnTh[:, 0:2 * P], xnTl[:, 0:2 * P]
        tgtT = sum_r
        xmh, xml = sb("xmh", 2 * S, F32R), sb("xml", 2 * S, F32R)
        qkw, qkwT = xn[0][:, 0:4 * D], xn[0][:, 4 * D:8 * D]
        scratch = sb("scratch", 5 * S + 2 * TB * QG * P)
        p1 = [scratch[:, i * S:(i + 1) * S] for i in range(3)]
        p2 = [scratch[:, (3 + i) * S:(4 + i) * S] for i in range(2)]
        dT = [scratch[:, 5 * S + g * TB * QG * P:5 * S + (g + 1) * TB * QG * P] for g in range(2)]
        at = [0]

        def lent(n):
            at[0] += n
            return scratch[:, at[0] - n:at[0]]

        xt, hs, hT, ys = lent(RING * ROW), lent(2 * F), lent(2 * F), lent(RING * D)
        cmp1, cmp2 = lent(E * NT)[0:1, :], lent(SLOTS * E)[0:1, :]
        eidf, offf, roff = (lent(SLOTS)[0:1, :] for _ in range(3))
        more_rows = scratch[:, 2 * E * F:2 * E * F + 2 * TB * 2 * ROW]
        raw1, raw2 = scratch[:, 0:E * F], scratch[:, E * F:2 * E * F]
        zb = sb("zb", PAIRS * D)
        zs = [zb] + [scratch[:, i * PAIRS * D:(i + 1) * PAIRS * D] for i in range(BATCHES - 1)]
        sums = [sum_r] + [scratch[:, 3 * PAIRS * D + i * TB * D:3 * PAIRS * D + (i + 1) * TB * D] for i in range(BATCHES - 1)]
        mx, nb = sb("mx", 2 * TB), sb("nb", 2 * TB)
        l1, l2 = sb("l1", TB), sb("l2", TB)
        r1, r2, cc = sb("r1", TB), sb("r2", TB), sb("cc", TB)
        oT = [t[:, 0:QG * P] for t in dT]
        ss, so = sb("ss", TB), sb("so", TB)

        (router_loaded, router_ready, w_loaded, small_loaded, masks_made, pool_step, dve_step, wT_ps, w_half, w1_sb, w2_sb, wr_ps,
         lam_in, lam_ps, lam_exp, ln_stats, ln_rstd, rows_ready, rows_copied, tgtT_ps, tgtT_sb, logits_ps, lg_read,
         gap_ready, gap_exp, cnt_ready, prefix_ps, slots_ready, table_ready, pads_sent,
         xT_ps, xh_ready, xl_ready, h_ps, h_sb, hT_ps, hT_sb, y_ps, y_sb,
         z_used, xn_ready, xnT_ps, xnTh_sb, xnTl_sb, qkT_ps, qkT_sb, M_ps, M_sb, xm_ps, xmh_sb, xml_sb,
         s_ps, nb_ready, p_ready, diff_ready, dT_ps, dT_sb, oT_ps, oT_sb, o_ps, values_added, beta_added,
         ss_ready, so_ready, weighted, token_added, scaled, gained, merged, x_done, stored) = (sem(n) for n in (
            "router_loaded", "router_ready", "w_loaded", "small_loaded", "masks_made", "pool_step", "dve_step", "wT_ps", "w_half",
            "w1_sb", "w2_sb", "wr_ps", "lam_in", "lam_ps", "lam_exp", "ln_stats", "ln_rstd", "rows_ready",
            "rows_copied", "tgtT_ps", "tgtT_sb", "logits_ps", "lg_read", "gap_ready", "gap_exp", "cnt_ready",
            "prefix_ps", "slots_ready", "table_ready", "pads_sent", "xT_ps", "xh_ready",
            "xl_ready", "h_ps", "h_sb", "hT_ps", "hT_sb", "y_ps", "y_sb", "z_used", "xn_ready",
            "xnT_ps", "xnTh_sb", "xnTl_sb", "qkT_ps", "qkT_sb", "M_ps", "M_sb", "xm_ps", "xmh_sb", "xml_sb",
            "s_ps", "nb_ready", "p_ready", "diff_ready", "dT_ps", "dT_sb", "oT_ps", "oT_sb", "o_ps",
            "values_added", "beta_added", "ss_ready", "so_ready", "weighted", "token_added", "scaled", "gained", "merged", "x_done", "stored"))
        zs_loaded = [None] + [sem(f"zs_loaded{b}") for b in range(1, BATCHES)]
        x_loaded = [sem(f"x_loaded{b}") for b in range(BATCHES)]
        xt_loaded = [sem(f"xt_loaded{r}") for r in range(RING)]
        rows_sent = [sem(f"rows_sent{par}") for par in range(2)]
        went_by = sem("went_by")
        z_loaded = [sem(f"z_loaded{h}") for h in range(2)]
        y_sent = [sem(f"y_sent{r}") for r in range(RING)]

        x_v = x_in.rearrange("b (p j) d -> b p (j d)", p=P)
        out_v = out.rearrange("b (p j) d -> b p (j d)", p=P)
        results_v = results.rearrange("(b p j) d -> b p (j d)", p=P, b=BATCHES)
        row_places = [t.rearrange("p (j k r) -> p j k r", j=TB, k=2)
                      for t in (rowbuf[:, 0:TB * 2 * ROW], rowbuf[:, TB * 2 * ROW:], more_rows[:, 0:TB * 2 * ROW], more_rows[:, TB * 2 * ROW:])]

        def rows_bank(a):
            return 6 if a < BATCHES else 7

        def rows_of(p, b):
            return row_places[b % 2 if p else b]

        mv = [mvs[:, i * 2 * TB:(i + 1) * 2 * TB].rearrange("p (j c) -> p j c", c=2) for i in range(LN)]
        rs, nm = ([t[:, i * TB:(i + 1) * TB] for i in range(LN)] for t in (rss, nms))
        bias_v = biases[:, :].rearrange("p (e c) -> p e c", e=E)
        dest_v = dest[:, :].rearrange("p (t k) -> p t k", k=2)
        assert BATCHES == 4
        slot_v = slot[:, :].rearrange("p (a j k) -> p a j k", a=2, k=2)
        xt_v = xt.rearrange("p (r c) -> p r c", r=RING)

        def by_expert(t):
            return t[:, :].rearrange("p (e t) -> p e t", e=E)

        def by_tile(t):
            return t[:, :].rearrange("p (e t) -> p t e", e=E)

        def over_experts(t):
            return t[:, :].unsqueeze(2).broadcast_to([P, TB, E])

        def over_tiles(t):
            return t[:, :].unsqueeze(2).broadcast_to([P, E, TB])

        def expert_offsets(eng, table, step, at, s, n):
            _, values = nc.values_load_multi_w_load_instructions(
                table[0:1, s:s + n] if isinstance(s, int) else table[0:1, bass.ds(s, n)], engines=[eng], min_val=0, max_val=(E - 1) * step,
                skip_runtime_bounds_check_because="VectorE clamps the table to the last expert")
            return {at + i: value for i, value in enumerate(values)}

        N_SMALL = 10
        GROUPS = TB // QG

        def wait_apart(eng, *waits):
            for sem, v in waits:
                eng.wait_ge(sem, v)
            eng.sem_inc(went_by, 1)

        block = ctx.enter_context(nc.Block())

        @block.sync
        def _(sp):
            for b in range(BATCHES):
                sp.dma_start(x[:, b * TB * D:(b + 1) * TB * D], x_v[b]).then_inc(x_loaded[b], 16)
            sp.dma_start(raw2.rearrange("d (e f) -> d e f", e=E), W2.rearrange("e d f -> d e f")).then_inc(w_loaded, 16)

            def experts(p):
                if p == 0:
                    sp.wait_ge(masks_made, 1)
                    sp.dma_start(rows[E * REGION:, :], padrows[:, :]).then_inc(pads_sent, 16)
                sp.wait_ge(table_ready, p + 1)
                for e in range(E):
                    at = sp.value_load(carry_i[0:1, e:e + 1], min_val=0, max_val=E * REGION)
                    sp.dma_start(rows[bass.ds(at, P), :], padrows[:, :]).then_inc(pads_sent, 16)
                sp.wait_ge(pads_sent, 16 * (1 + E * (p + 1)))
                for par in range(2):
                    sp.wait_ge(rows_sent[par], 16 * PAIRS * BATCHES // 2 * (p + 1))

                def load(lap, r, again):
                    s = lap * RING + r
                    at = sp.value_load(row_of[0:1, bass.ds(s, 1)], min_val=0, max_val=E * REGION)
                    if again:
                        wait_apart(sp, (xT_ps, SLOTS * p + s - RING + 1))
                        wait_apart(sp, (y_sent[r], 16 * (LAPS * p + lap)))
                    sp.dma_start(xt[:, r * ROW:(r + 1) * ROW], rows[bass.ds(at, P), :]).then_inc(xt_loaded[r], 16)

                for r in range(RING):
                    load(0, r, p > 0)
                with sp.Fori(1, LAPS) as lap:
                    for r in range(RING):
                        load(lap, r, True)
                for r in range(RING):
                    sp.wait_ge(y_sent[r], 16 * LAPS * (p + 1))

            experts(0)
            for b in range(BATCHES):
                for h in range(2):
                    n = 2 * b + h
                    if n >= 2:
                        sp.wait_ge(z_used, n - 1)
                    c = slice(h * TB * D, (h + 1) * TB * D)
                    sp.dma_start(zb[:, c], results_v[b][:, c]).then_inc(z_loaded[h], 16)
            experts(1)
            for h in range(2):
                c = slice(h * TB * D, (h + 1) * TB * D)
                sp.dma_start(zb[:, c], results_v[0][:, c]).then_inc(z_loaded[h], 16)
            for b in range(1, BATCHES):
                sp.dma_start(zs[b][:, :], results_v[b]).then_inc(zs_loaded[b], 16)
            for b in range(BATCHES):
                sp.wait_ge(x_done, b + 1)
                sp.dma_start(out_v[b], x[:, b * TB * D:(b + 1) * TB * D]).then_inc(stored, 16)
            sp.wait_ge(stored, 16 * BATCHES)

        @block.gpsimd
        def _(pool):
            steps = Steps(pool, pool_step)
            pool.memset(ident[:, :], 0.0)
            pool.memset(upper[:, :], 1.0)
            pool.memset(ones[:, :], 1.0)
            pool.memset(nhalf[:, :], -0.5)
            pool.memset(onesE[:, :], 1.0)
            pool.memset(padrows[:, :], 0.0)
            pool.memset(segm[:, :], 1.0)
            pool.iota(dest[:, :], [[2 * S, BATCHES], [2, TB], [1, 2]], base=0, channel_multiplier=2 * TB)
            pool.iota(base[:, :], [[REGION, E]], base=0, channel_multiplier=0, allow_small_or_imprecise_dtypes=True)
            pool.iota(first[:, :], [[-1, E], [0, TB]], base=E, channel_multiplier=0, allow_small_or_imprecise_dtypes=True)
            pool.iota(tile128[:, :], [[P, NT]], base=0, channel_multiplier=0, allow_small_or_imprecise_dtypes=True)
            steps.then(pool.iota(sidx[:, :], [[1, SLOTS]], base=0, channel_multiplier=0, allow_small_or_imprecise_dtypes=True))
            pool.affine_select(out=ident[:, :], in_=ident[:, :], compare_op=ALU.not_equal, fill=1.0, base=0,
                               pattern=[[-1, P]], channel_multiplier=1)
            pool.affine_select(out=upper[:, :], in_=upper[:, :], compare_op=ALU.is_gt, fill=0.0, base=0,
                               pattern=[[1, P]], channel_multiplier=-1)
            pool.iota(padrows[:, D:ROW].bitcast(I32), [[0, 1]], base=2 * N, channel_multiplier=1)
            steps.then(pool.affine_select(out=by_expert(segm), in_=by_expert(segm), compare_op=ALU.not_equal, fill=0.0, base=0,
                                          pattern=[[0, E], [1, TB]], channel_multiplier=0))
            pool.nop().then_inc(masks_made, 1)

            def rstd(n):
                wait_apart(pool, (ln_stats, n + 1))
                steps.then(pool.tensor_scalar(rs[n % LN], mv[n % LN][:, :, 1], EPS, 0.0, ALU.add, ALU.add))
                steps.then(pool.tensor_tensor(rs[n % LN], rs[n % LN], nhalf[:, :], ALU.pow))
                steps.then(pool.tensor_tensor(nm[n % LN], mv[n % LN][:, :, 0], rs[n % LN], ALU.mult))
                pool.tensor_scalar(nm[n % LN], nm[n % LN], -1.0, 0.0, ALU.mult, ALU.add).then_inc(ln_rstd, 1)

            def add_beta(p):
                pool.wait_ge(rows_ready, BATCHES * (p + 1))
                for b in range(BATCHES):
                    xb = x[:, b * TB * D:(b + 1) * TB * D].rearrange("p (j d) -> p j d", j=TB)
                    pool.tensor_tensor(xb, xb, betab[:, :].unsqueeze(1).broadcast_to([P, TB, D]), ALU.add).then_inc(beta_added, 1)

            def scatter(p, b, tiles=range(TB)):
                if tiles[0] == 0:
                    wait_apart(pool, (slots_ready, BATCHES * p + b + 1), (rows_copied, BATCHES * p + b + 1))
                for j in tiles:
                    for k in range(2):
                        pool.indirect_dma_start(rows, bass.IndirectOffsetOnAxis(slot_v[:, b % 2, j, k:k + 1], 0),
                                                rows_of(p, b)[:, j, k, :], None).then_inc(rows_sent[b % 2], 16)

            def experts(p):
                def send(lap, r):
                    wait_apart(pool, (y_sb, SLOTS * p + lap * RING + r + 1))
                    pool.indirect_dma_start(results, bass.IndirectOffsetOnAxis(xt_v[:, r, D:ROW].bitcast(I32), 0),
                                            ys[:, r * D:(r + 1) * D], None, bounds_check=2 * N - 1,
                                            oob_is_err=False).then_inc(y_sent[r], 16)
                with pool.Fori(0, LAPS) as lap:
                    for r in range(RING):
                        send(lap, r)

            def value_scale(b, g):
                pool.wait_ge(ss_ready, GROUPS * b + g + 1)
                part = slice(g * QG, (g + 1) * QG)
                steps.then(pool.tensor_scalar(so[:, part], ss[:, part], OUT_GAIN / D, OUT_GAIN * EPS, ALU.mult, ALU.add))
                steps.then(pool.tensor_tensor(so[:, part], so[:, part], nhalf[:, 0:QG], ALU.pow))
                pool.tensor_tensor(so[:, part], so[:, part], r1[:, part], ALU.mult).then_inc(so_ready, 1)

            def merge_add(b):
                pool.wait_ge(scaled, b)
                rb = sum_r[:, :].rearrange("p (j d) -> p j d", j=TB)
                steps.then(pool.tensor_tensor(rb, rb, gammab[:, :].unsqueeze(1).broadcast_to([P, TB, D]), ALU.mult))
                pool.wait_ge(beta_added, b + 1)
                xb = x[:, b * TB * D:(b + 1) * TB * D]
                pool.tensor_tensor(xb, xb, sum_r[:, :], ALU.add).then_inc(merged, 1)

            def add_tokens(b):
                pool.wait_ge(weighted, b)
                pool.tensor_tensor(sums[b][:, :], sums[b][:, :], tgt[:, b * TB * D:(b + 1) * TB * D], ALU.add).then_inc(token_added, 1)

            for b in range(BATCHES):
                rstd(b)
            for b in range(BATCHES):
                scatter(0, b)
            add_beta(0)
            experts(0)

            n = BATCHES
            for _ in range(2):
                rstd(n)
                n += 1
            for b in range(BATCHES):
                if b > 1:
                    scatter(1, b - 2, range(TB // 2))
                if b < BATCHES - 1:
                    rstd(n)
                    n += 1
                    merge_add(b + 1)
                if b:
                    value_scale(b - 1, 1)
                if b > 1:
                    scatter(1, b - 2, range(TB // 2, TB))
                for _ in range((b > 0) + (b < BATCHES - 1)):
                    rstd(n)
                    n += 1
                value_scale(b, 0)
            scatter(1, BATCHES - 2, range(TB // 2))
            value_scale(BATCHES - 1, 1)
            rstd(n)
            assert n == 4 * BATCHES - 1
            scatter(1, BATCHES - 2, range(TB // 2, TB))
            scatter(1, BATCHES - 1)
            add_beta(1)
            experts(1)
            for b in (1, 2):
                add_tokens(b)
            for b in range(BATCHES):
                rstd(4 * BATCHES + b)
                if b == 0:
                    add_tokens(3)
                if b:
                    pool.wait_ge(scaled, BATCHES - 1 + b)
                    rb = sums[b - 1][:, :].rearrange("p (j d) -> p j d", j=TB)
                    pool.tensor_tensor(rb, rb, gammab[:, :].unsqueeze(1).broadcast_to([P, TB, D]), ALU.mult).then_inc(gained, 1)

        @block.scalar
        def _(act):
            act.dma_start(wr[:, :], Wr).then_inc(router_loaded, 16)
            act.dma_start(b1r, b1.rearrange("e (c f) -> (e c) f", f=P)).then_inc(router_loaded, 16)
            act.dma_start(brb[:, :], br.partition_broadcast(P)).then_inc(router_loaded, 16)
            act.dma_start(qkw[:, 0:2 * D], w_q12).then_inc(small_loaded, 16)
            act.dma_start(qkw[:, 2 * D:4 * D], w_k12).then_inc(small_loaded, 16)
            act.dma_start(wv[:, :], w_v).then_inc(small_loaded, 16)
            for i, l in enumerate((lq1, lk1, lq2, lk2)):
                act.dma_start(lamv[:, i:i + 1], l.rearrange("(d a) -> d a", a=1)).then_inc(small_loaded, 16)
            act.dma_start(gammab[:, :], gamma.partition_broadcast(P)).then_inc(small_loaded, 16)
            act.dma_start(betab[:, :], beta.partition_broadcast(P)).then_inc(small_loaded, 16)
            act.dma_start(bias_v[:, :, FC:BIAS], b2.partition_broadcast(P)).then_inc(small_loaded, 16)
            act.dma_start(raw1.rearrange("f (g d) -> f g d", d=D), W1.rearrange("e (c f) d -> f (e c) d", f=P)).then_inc(w_loaded, 16)

            def weights(experts):
                for g in experts:
                    act.wait_ge(wT_ps, 2 * g + 1)
                    act.activation(w1h[:, g * F:(g + 1) * F], bank(g % 2), ACT.Copy).then_inc(w_half, 1)
                    act.wait_ge(wT_ps, 2 * g + 2)
                    act.activation(w2T[:, g * F:(g + 1) * F], bank(2 + g % 2), ACT.Copy).then_inc(w2_sb, 1)

            def normalise(dst, src, n):
                act.wait_ge(ln_rstd, n + 1)
                for j in range(TB):
                    ins = act.activation(dst(j), src[:, j * D:(j + 1) * D], ACT.Identity, scale=rs[n % LN][:, j:j + 1], bias=nm[n % LN][:, j:j + 1])
                return ins

            def make_rows(p, b, n):
                if p:
                    act.wait_ge(rows_sent[b % 2], 16 * PAIRS * (BATCHES // 2 + b // 2))
                normalise(lambda j: rows_of(p, b)[:, j, 0, 0:D], x[:, b * TB * D:(b + 1) * TB * D], n).then_inc(rows_ready, 1)

            def make_xn(b, n):
                normalise(lambda j: xn[b % 2][:, j * D:(j + 1) * D], x[:, b * TB * D:(b + 1) * TB * D], n).then_inc(xn_ready, 1)

            def copy_rows(p, b):
                act.wait_ge(rows_ready, BATCHES * p + b + 1)
                rb = rows_of(p, b)[:, :, 0, 0:D]
                act.activation(rows_of(p, b)[:, :, 1, 0:D], rb, ACT.Copy)
                act.activation(tgt[:, b * TB * D:(b + 1) * TB * D].rearrange("p (j d) -> p j d", j=TB), rb, ACT.Copy).then_inc(rows_copied, 1)

            def copy_tgtT(a, i):
                act.wait_ge(tgtT_ps, 2 * a + i + 1)
                act.activation(tgtT[:, i * 512:(i + 1) * 512], bank(rows_bank(a)), ACT.Copy).then_inc(tgtT_sb, 1)

            def gap(a):
                act.wait_ge(gap_ready, a + 1)
                act.activation(ex[:, :], ex[:, :], ACT.Exp).then_inc(gap_exp, 1)

            def experts(p):
                def xh_part(s, u):
                    g = SLOTS * p + s
                    act.wait_ge(xT_ps, g + 1)
                    if p or not isinstance(s, int) or s >= 2:
                        act.wait_ge(h_ps, g - 1)
                    act.activation(xh[:, (u % 2) * P:(u % 2 + 1) * P], bank(u % 2, 0, P), ACT.Copy).then_inc(xh_ready, 1)

                def h_copy(s, u):
                    g, k = SLOTS * p + s, u % 2
                    act.wait_ge(h_ps, g + 1)
                    if p or not isinstance(s, int) or s >= 2:
                        act.wait_ge(hT_ps, g - 1)
                    act.activation(hs[:, k * F:(k + 1) * F], bank(2 + k), ACT.Copy).then_inc(h_sb, 1)

                xh_part(0, 0)
                for s in range(2):
                    xh_part(s + 1, s + 1)
                    h_copy(s, s)
                with act.Fori(1, SLOTS // 2 - 1) as i:
                    for u in range(2):
                        xh_part(i * 2 + u + 1, u + 1)
                        h_copy(i * 2 + u, u)
                xh_part(SLOTS - 1, 1)
                h_copy(SLOTS - 2, 0)
                h_copy(SLOTS - 1, 1)

            def copy_xnT(b):
                act.wait_ge(xnT_ps, b + 1)
                act.activation(xnTh[:, :], banks[:, 4 * 512:6 * 512], ACT.Copy).then_inc(xnTh_sb, 1)

            def copy_xm(b):
                for m in range(4):
                    act.wait_ge(xm_ps, 4 * b + m + 1)
                    act.activation(xmh[:, m * 512:(m + 1) * 512], bank(m), ACT.Copy).then_inc(xmh_sb, 1)

            def dT_copy(b, i):
                act.wait_ge(dT_ps, TB * b + i + 1)
                if b and i % QG == 0:
                    act.wait_ge(oT_ps, GROUPS * (b - 1) + i // QG + 1)
                act.activation(dT[i // QG].rearrange("p (k q) -> p k q", k=TB)[:, :, (i % QG) * P:(i % QG + 1) * P],
                               banks[:, 4 * 512:6 * 512].rearrange("p (k q) -> p k q", k=TB), ACT.Copy).then_inc(dT_sb, 1)

            def o_copy(b, g):
                act.wait_ge(oT_ps, GROUPS * b + g + 1)
                act.activation(oT[g], bank(6), ACT.Copy).then_inc(oT_sb, 1)

            def squares(b, g):
                act.wait_ge(o_ps, GROUPS * b + g + 1)
                for q in range(QG):
                    i = g * QG + q
                    ins = act.activation(oT[g][:, q * D:(q + 1) * D], bank(6, q * P, (q + 1) * P), ACT.Square,
                                         scale=r1[:, i:i + 1], accum_out=ss[:, i:i + 1])
                ins.then_inc(ss_ready, 1)

            def attention(b, n):
                def probabilities(i):
                    t = TB * b + i
                    for m, (pp, ll) in enumerate(((p1[t % 3], l1), (p2[t % 2], l2))):
                        act.wait_ge(nb_ready, 2 * t + m + 1)
                        if m == 0 and t >= 3:
                            act.wait_ge(dT_ps, t - 2)
                        if m == 1 and t >= 2:
                            act.wait_ge(diff_ready, t - 1)
                        act.activation(pp, banks[:, 2 * m * 512:(2 * m + 2) * 512], ACT.Exp,
                                       bias=nb[:, 2 * i + m:2 * i + m + 1], scale=SCALE,
                                       accum_out=ll[:, i:i + 1]).then_inc(p_ready, 1)

                last, after = b > 0, b < BATCHES - 1
                a = BATCHES + b - 1
                for i in range(TB):
                    probabilities(i)
                    if last and i == 0:
                        dT_copy(b - 1, TB - 1)
                    if last and i == 2:
                        o_copy(b - 1, 1)
                    if after and i == 2:
                        normalise(lambda j: sum_r[:, j * D:(j + 1) * D], sum_r, n).then_inc(scaled, 1)
                    if last and i == 3:
                        squares(b - 1, 1)
                    if i >= 2:
                        dT_copy(b, i - 2)
                    if last and i == 5:
                        make_rows(1, b - 1, n + after)
                    if after and i == 6:
                        make_xn(b + 1, n + after + last)
                    if last and i == 6:
                        copy_tgtT(a, 0)
                if last:
                    copy_tgtT(a, 1)
                o_copy(b, 0)
                if after:
                    copy_xnT(b + 1)
                squares(b, 0)
                dT_copy(b, TB - 2)
                if after:
                    copy_xm(b + 1)
                if last:
                    gap(a)
                    copy_rows(1, b - 1)
                return n + 2 * after + last

            def turned_rows(p, b, n):
                make_rows(p, b, n)
                for i in range(2):
                    copy_tgtT(BATCHES * p + b, i)
                copy_rows(p, b)

            act.wait_ge(wr_ps, 1)
            turned_rows(0, 0, 0)
            for b in range(BATCHES):
                if b == 0:
                    gap(b)
                if b + 1 < BATCHES:
                    turned_rows(0, b + 1, b + 1)
                if b:
                    gap(b)
                if 0 < b < 3:
                    weights(range((b - 1) * E // 2, b * E // 2))
            act.wait_ge(lam_ps, 1)
            act.activation(lame[:, :], bank(5, 0, 2), ACT.Exp).then_inc(lam_exp, 1)
            experts(0)
            n = BATCHES + 1
            make_xn(0, n)
            copy_xnT(0)
            copy_xm(0)
            n += 1
            for b in range(BATCHES):
                n = attention(b, n)
            dT_copy(BATCHES - 1, TB - 1)
            o_copy(BATCHES - 1, 1)
            squares(BATCHES - 1, 1)
            turned_rows(1, BATCHES - 1, n)
            gap(2 * BATCHES - 1)
            experts(1)
            for b in range(1, BATCHES):
                act.wait_ge(zs_loaded[b], 16)
                for j in range(TB):
                    c = (b * TB + j) * 2
                    ins = act.activation(sums[b][:, j * D:(j + 1) * D], zs[b][:, 2 * j * D:(2 * j + 1) * D], ACT.Copy, scale=wts[:, c:c + 1])
                ins.then_inc(weighted, 1)
            for b in range(BATCHES - 1):
                normalise(lambda j: sums[b][:, j * D:(j + 1) * D], sums[b], 4 * BATCHES + b).then_inc(scaled, 1)

        @block.tensor
        def _(pe):
            def three(o, ah, al, bh, bl):
                pe.matmul(o, ah, bh, start=True, stop=False)
                pe.matmul(o, ah, bl, start=False, stop=False)
                return pe.matmul(o, al, bh, start=False, stop=True)

            def router_weights():
                pe.wait_ge(masks_made, 1)
                pe.wait_ge(router_loaded, 48)
                pe.transpose(bank(4, 0, E), wr[:, :], ident[0:E, 0:E])
                pe.transpose(bank(4, E, E + E * FC), b1r, ident[0:E * FC, 0:E * FC]).then_inc(wr_ps, 1)

            def weights(experts):
                pe.wait_ge(w_loaded, 32)
                for g in experts:
                    if g >= 2:
                        pe.wait_ge(w1_sb, g - 1)
                        pe.wait_ge(w2_sb, g - 1)
                    for c in range(FC):
                        k = g * FC + c
                        ins = pe.transpose(bank(g % 2, c * P, (c + 1) * P), raw1[:, k * D:(k + 1) * D], ident[:, :])
                    ins.then_inc(wT_ps, 1)
                    for c in range(FC):
                        k = g * FC + c
                        ins = pe.transpose(bank(2 + g % 2, c * P, (c + 1) * P), raw2[:, k * P:(k + 1) * P], ident[:, :])
                    ins.then_inc(wT_ps, 1)

            def turn_rows(a, i):
                pe.wait_ge(rows_ready, a + 1)
                if i:
                    pe.wait_ge(tgtT_sb, 2 * a + 1)
                elif a:
                    pe.wait_ge(tgtT_sb, 2 * a)
                    if rows_bank(a) == 7:
                        pe.wait_ge(slots_ready, a)
                for j in range(4):
                    ins = pe.transpose(bank(rows_bank(a), j * P, (j + 1) * P), rows_of(*divmod(a, BATCHES))[:, 4 * i + j, 0, 0:D], ident[:, :])
                ins.then_inc(tgtT_ps, 1)

            def logits(a):
                pe.wait_ge(tgtT_sb, 2 * a + 2)
                if a:
                    pe.wait_ge(slots_ready, a)
                lo = bank(7, 0, G).rearrange("p (e t) -> p e t", e=E)
                for j in range(TB):
                    ins = pe.matmul(lo[:, :, j], tgtT[:, j * P:(j + 1) * P], wrT[:, :], start=True, stop=True)
                ins.then_inc(logits_ps, 1)

            def prefix(a):
                pe.wait_ge(cnt_ready, a + 1)
                pe.matmul(bank(7, 0, G), upper[:, :], cnt[:, :], start=True, stop=True)
                pe.matmul(bank(7, G, 2 * G), ones[:, :], cnt[:, :], start=True, stop=True).then_inc(prefix_ps, 1)

            def experts(p):
                def later(s, n):
                    return p > 0 or not isinstance(s, int) or s >= n

                def turn_x(s, u):
                    g, r = SLOTS * p + s, u % RING
                    lap = s // RING if isinstance(s, int) else s_lap[0] + u // RING
                    pe.wait_ge(xt_loaded[r], 16 * (LAPS * p + lap + 1))
                    if later(s, 2):
                        pe.wait_ge(xl_ready, g - 1)
                    pe.transpose(bank(u % 2, 0, P), xt_v[:, r, 0:D], ident[:, :]).then_inc(xT_ps, 1)

                def first(s, u):
                    g, k = SLOTS * p + s, u % 2
                    pe.wait_ge(xl_ready, g + 1)
                    if later(s, 2):
                        pe.wait_ge(h_sb, g - 1)
                    three(bank(2 + k), xh[:, k * P:(k + 1) * P], xl[:, k * P:(k + 1) * P],
                          w1h[:, bass.ds(w_at[u], F)], w1l[:, bass.ds(w_at[u], F)]).then_inc(h_ps, 1)

                def turn_h(s, u):
                    g, k = SLOTS * p + s, u % 2
                    pe.wait_ge(h_sb, g + 1)
                    if later(s, 2):
                        pe.wait_ge(hT_sb, g - 1)
                    for c in range(FC):
                        ins = pe.transpose(bank(4 + k, c * P, (c + 1) * P), hs[:, k * F + c * P:k * F + (c + 1) * P], ident[:, :])
                    ins.then_inc(hT_ps, 1)

                def second(s, u):
                    g, k = SLOTS * p + s, u % 2
                    pe.wait_ge(hT_sb, g + 1)
                    if later(s, 2):
                        pe.wait_ge(y_sb, g - 1)
                    for c in range(FC):
                        ins = pe.matmul(bank(6 + k, 0, D), hT[:, k * F + c * P:k * F + (c + 1) * P],
                                        w2T[:, c * D:][:, bass.ds(w_at[u], D)], start=(c == 0), stop=(c == FC - 1))
                    ins.then_inc(y_ps, 1)

                def step(s, u):
                    known = isinstance(s, int)
                    if not known or s + 2 < SLOTS:
                        turn_x(s + 2, u + 2)
                    if not known or 0 <= s + 1 < SLOTS:
                        first(s + 1, u + 1)
                    if not known or 0 <= s < SLOTS:
                        turn_h(s, u)
                    if not known or s >= 1:
                        second(s - 1, u - 1)

                s_lap, w_at = [0], {}
                w_at.update(expert_offsets(PE, weights_at, F, 0, 0, 4))
                for s in range(-2, 3):
                    step(s, s)
                with pe.Fori(0, LAPS - 1) as lap:
                    s_lap[0] = lap
                    w_at.update(expert_offsets(PE, weights_at, F, 0, lap * RING, RING + 4))
                    for u in range(3, RING + 3):
                        step(lap * RING + u, u)
                tail = (LAPS - 1) * RING
                w_at.update(expert_offsets(PE, weights_at, F, tail, tail, RING))
                for s in range(tail + 3, SLOTS + 1):
                    step(s, s)

            def turn_xn(b):
                pe.wait_ge(xn_ready, b + 1)
                if b:
                    pe.wait_ge(dT_sb, TB * b - 2)
                for t in range(TB):
                    ins = pe.transpose(bank(4 + t // 4, (t % 4) * P, (t % 4 + 1) * P), xn[b % 2][:, t * D:(t + 1) * D], ident[:, :])
                ins.then_inc(xnT_ps, 1)

            def multiply_M(b):
                pe.wait_ge(xnTh_sb, b + 1)
                pe.wait_ge(xnTl_sb, b + 1)
                for m in range(4):
                    if b:
                        pe.wait_ge(p_ready, 2 * TB * b - 1 + m // 2)
                    c, h = slice((m // 2) * D, (m // 2 + 1) * D), slice((m % 2) * 512, (m % 2 + 1) * 512)
                    three(bank(m), Mh[:, c], Ml[:, c], xnTh[:, h], xnTl[:, h]).then_inc(xm_ps, 1)

            def scores(b, i):
                for m in range(2):
                    if i:
                        pe.wait_ge(p_ready, 2 * (TB * b + i) + m - 1)
                    for h in range(2):
                        c, k = slice(m * S + i * P, m * S + (i + 1) * P), slice(h * 512, (h + 1) * 512)
                        ins = three(bank(2 * m + h), xmh[:, c], xml[:, c], xnTh[:, k], xnTl[:, k])
                    ins.then_inc(s_ps, 1)

            def turn(b, i):
                t = TB * b + i
                pe.wait_ge(diff_ready, t + 1)
                if t:
                    pe.wait_ge(dT_sb, t)
                for k in range(TB):
                    ins = pe.transpose(bank(4 + k // 4, (k % 4) * P, (k % 4 + 1) * P), p1[t % 3][:, k * P:(k + 1) * P], ident[:, :])
                ins.then_inc(dT_ps, 1)

            def values(b, g, half):
                if half == 0:
                    pe.wait_ge(dT_sb, TB * b + (g + 1) * QG)
                    if GROUPS * b + g:
                        pe.wait_ge(values_added, GROUPS * b + g)
                for k in range(half * TB // 2, (half + 1) * TB // 2):
                    ins = pe.matmul(bank(6), xn[b % 2][:, k * D:(k + 1) * D], dT[g][:, k * QG * P:(k + 1) * QG * P],
                                    start=(k == 0), stop=(k == TB - 1))
                if half:
                    ins.then_inc(oT_ps, 1)

            def multiply_Wv(b, g):
                pe.wait_ge(oT_sb, GROUPS * b + g + 1)
                for q in range(QG):
                    ins = pe.matmul(bank(6, q * P, (q + 1) * P), oT[g][:, q * P:(q + 1) * P], wv[:, :], start=True, stop=True)
                ins.then_inc(o_ps, 1)

            def attention(b):
                last, after = b > 0, b < BATCHES - 1
                a = BATCHES + b - 1
                pe.wait_ge(xmh_sb, 4 * b + 4)
                pe.wait_ge(xml_sb, 4 * b + 4)
                for i in range(TB):
                    scores(b, i)
                    if last and i == 0:
                        turn(b - 1, TB - 1)
                    if last and i in (1, 2):
                        values(b - 1, 1, i - 1)
                    if last and i == 3:
                        multiply_Wv(b - 1, 1)
                    if i >= 2:
                        turn(b, i - 2)
                    if last and i in (6, 7):
                        turn_rows(a, i - 6)
                    if i in (6, 7):
                        values(b, 0, i - 6)
                if last:
                    logits(a)
                if after:
                    turn_xn(b + 1)
                multiply_Wv(b, 0)
                if after:
                    pe.wait_ge(xnTh_sb, b + 2)
                    pe.wait_ge(xnTl_sb, b + 2)
                turn(b, TB - 2)
                if after:
                    multiply_M(b + 1)
                if last:
                    pe.wait_ge(lg_read, a + 1)
                    prefix(a)

            router_weights()
            pe.wait_ge(router_ready, 1)
            for i in range(2):
                turn_rows(0, i)
            for b in range(BATCHES):
                logits(b)
                if b == 0:
                    prefix(b)
                if b + 1 < BATCHES:
                    for i in range(2):
                        turn_rows(b + 1, i)
                if b:
                    prefix(b)
                if 0 < b < 3:
                    weights(range((b - 1) * E // 2, b * E // 2))
            pe.wait_ge(lam_in, 1)
            pe.matmul(bank(5, 0, 2), ones[:, :], lamp[:, :], start=True, stop=True).then_inc(lam_ps, 1)
            pe.wait_ge(w1_sb, E)
            pe.wait_ge(w2_sb, E)
            pe.wait_ge(small_loaded, 16 * N_SMALL)
            for m in range(4):
                ins = pe.transpose(bank(4, m * D, (m + 1) * D), qkw[:, m * D:(m + 1) * D], ident[:, :])
            ins.then_inc(qkT_ps, 1)
            pe.wait_ge(qkT_sb, 1)
            for m in range(2):
                ins = pe.matmul(bank(3, m * D, (m + 1) * D), qkwT[:, m * D:(m + 1) * D], qkwT[:, (2 + m) * D:(3 + m) * D], start=True, stop=True)
            ins.then_inc(M_ps, 1)
            pe.wait_ge(M_sb, 1)
            pe.wait_ge(lam_exp, 1)
            pe.wait_ge(table_ready, 1)
            experts(0)
            turn_xn(0)
            multiply_M(0)
            for b in range(BATCHES):
                attention(b)
            turn(BATCHES - 1, TB - 1)
            for half in range(2):
                values(BATCHES - 1, 1, half)
            multiply_Wv(BATCHES - 1, 1)
            for i in range(2):
                turn_rows(2 * BATCHES - 1, i)
            logits(2 * BATCHES - 1)
            prefix(2 * BATCHES - 1)
            pe.wait_ge(table_ready, 2)
            experts(1)

        @block.vector
        def _(dve):
            steps = Steps(dve, dve_step)

            def router_weights():
                dve.wait_ge(wr_ps, 1)
                dve.tensor_copy(wrT[:, :], bank(4, 0, E))
                dve.tensor_copy(bias_v[:, :, 0:FC], bank(4, E, E + E * FC).rearrange("p (e c) -> p e c", e=E))
                dve.tensor_copy(by_expert(brt), over_tiles(brb))
                dve.tensor_copy(carry[:, :], base[:, :]).then_inc(router_ready, 1)
                dve.wait_ge(router_ready, 1)

            def small_weights():
                dve.wait_ge(small_loaded, 16 * N_SMALL)
                dve.tensor_scalar(gammab[:, :], gammab[:, :], 0.5, None, ALU.mult)
                dve.tensor_scalar(betab[:, :], betab[:, :], 0.5, None, ALU.mult)
                dve.tensor_tensor(lamp[:, 0:1], lamv[:, 0:1], lamv[:, 1:2], ALU.mult)
                dve.tensor_tensor(lamp[:, 1:2], lamv[:, 2:3], lamv[:, 3:4], ALU.mult).then_inc(lam_in, 1)

            def weights(experts):
                for g in experts:
                    dve.wait_ge(w_half, g + 1)
                    dve.tensor_tensor(w1l[:, g * F:(g + 1) * F], bank(g % 2), w1h[:, g * F:(g + 1) * F].bitcast(F32),
                                      ALU.subtract).then_inc(w1_sb, 1)

            def minus_lambda():
                dve.wait_ge(lam_exp, 1)
                steps.then(dve.tensor_tensor(nlam[:, :], lame[:, 1:2], lame[:, 0:1], ALU.subtract))
                steps.then(dve.tensor_scalar(nlam[:, :], nlam[:, :], -LAMBDA_INIT, None, ALU.add))

            def linked(ins):
                ins.then_inc(dve_step, 1)
                steps.n += 1
                wait_apart(dve, (dve_step, steps.start + steps.n))

            def tile_stats(st, src, tiles=range(TB)):
                for j in tiles:
                    ins = dve.bn_stats(st[:, j * 6:(j + 1) * 6], src(j))
                return ins

            def batch_stats(st, n):
                for j in range(TB):
                    ins = dve.bn_aggr(mv[n % LN][:, j, :], st[:, j * 6:(j + 1) * 6])
                ins.then_inc(ln_stats, 1)

            def x_tile(b):
                return lambda j: x[:, (b * TB + j) * D:(b * TB + j + 1) * D]

            def sum_tile(j):
                return sum_r[:, j * D:(j + 1) * D]

            def x_stats(b, n):
                if n:
                    dve.wait_ge(ln_stats, n)
                linked(tile_stats(st_x, x_tile(b)))
                batch_stats(st_x, n)

            def read_logits(a):
                dve.wait_ge(logits_ps, a + 1)
                dve.tensor_tensor(lg[:, :], bank(7, 0, G), brt[:, :], ALU.add).then_inc(lg_read, 1)

            def choose(a):
                dve.wait_ge(lg_read, a + 1)
                for m, oh in ((m1, oh1), (m2, oh2)):
                    steps.then(dve.tensor_reduce(m[:, :], by_tile(lg), AX_X, ALU.max))
                    steps.then(dve.tensor_tensor(by_tile(eq), by_tile(lg), over_experts(m), ALU.is_equal))
                    steps.then(dve.tensor_tensor(eq[:, :], eq[:, :], first[:, :], ALU.mult))
                    steps.then(dve.tensor_reduce(kk[:, :], by_tile(eq), AX_X, ALU.max))
                    steps.then(dve.tensor_tensor(by_tile(oh), by_tile(eq), over_experts(kk), ALU.is_equal))
                    if oh is oh1:
                        steps.then(dve.scalar_tensor_tensor(lg[:, :], oh1[:, :], -3.0e38, lg[:, :], ALU.mult, ALU.add))
                dve.tensor_tensor(cnt[:, :], oh1[:, :], oh2[:, :], ALU.add).then_inc(cnt_ready, 1)
                dve.tensor_tensor(ex[:, :], m2[:, :], m1[:, :], ALU.subtract).then_inc(gap_ready, 1)

            def place(a, b):
                par, p = b % 2, a // BATCHES
                if a >= 2:
                    dve.wait_ge(rows_sent[par], 16 * PAIRS * (a // 2))
                dve.tensor_copy(rows_of(p, b)[:, :, :, D].bitcast(I32), dest_v[:, b * TB:(b + 1) * TB, :])
                dve.wait_ge(gap_exp, a + 1)
                steps.then(dve.tensor_scalar(den[:, :], ex[:, :], 1.0, None, ALU.add))
                w = wts[:, b * 2 * TB:(b + 1) * 2 * TB].rearrange("p (t k) -> p t k", k=2)
                steps.then(dve.reciprocal(den[:, :], den[:, :]))
                dve.tensor_copy(w[:, :, 0], den[:, :])
                dve.tensor_tensor(w[:, :, 1], ex[:, :], den[:, :], ALU.mult)
                dve.wait_ge(prefix_ps, a + 1)
                steps.then(dve.tensor_tensor_scan(run[:, :], segm[:, :], bank(7, G, 2 * G), 0.0, ALU.mult, ALU.add))
                steps.then(dve.tensor_tensor(pos[:, :], run[:, :], bank(7, G, 2 * G), ALU.subtract))
                steps.then(dve.tensor_tensor(pos[:, :], pos[:, :], bank(7, 0, G), ALU.add))
                steps.then(dve.tensor_tensor(by_expert(pos), by_expert(pos), over_tiles(carry), ALU.add))
                steps.then(dve.tensor_tensor(carry[:, :], carry[:, :], by_expert(run)[:, :, TB - 1], ALU.add))
                sv = slotf[:, :].rearrange("p (t k) -> p t k", k=2)
                for k, oh in enumerate((oh1, oh2)):
                    steps.then(dve.tensor_tensor(eq[:, :], oh[:, :], pos[:, :], ALU.mult))
                    steps.then(dve.tensor_reduce(sv[:, :, k], by_tile(eq), AX_X, ALU.add))
                dve.tensor_copy(slot[:, par * 2 * TB:(par + 1) * 2 * TB], slotf[:, :]).then_inc(slots_ready, 1)

            def route(p, b):
                read_logits(BATCHES * p + b)
                choose(BATCHES * p + b)
                place(BATCHES * p + b, b)

            def table():
                dve.tensor_copy(carry_i[:, :], carry[:, :])
                steps.then(dve.tensor_tensor(carry[:, :], carry[:, :], base[:, :], ALU.subtract))
                c1 = cmp1[:, :].rearrange("p (e t) -> p e t", e=E)
                steps.then(dve.tensor_tensor(c1, carry[0:1, :].unsqueeze(2).broadcast_to([1, E, NT]),
                                             tile128[:, :].unsqueeze(1).broadcast_to([1, E, NT]), ALU.is_gt))
                steps.then(dve.tensor_reduce(ntile[:, :], c1, AX_X, ALU.add))
                steps.then(dve.tensor_tensor_scan(tend[:, :], onesE[:, :], ntile[:, :], 0.0, ALU.mult, ALU.add))
                c2 = cmp2[:, :].rearrange("p (s e) -> p s e", e=E)
                steps.then(dve.tensor_tensor(c2, sidx[:, :].unsqueeze(2).broadcast_to([1, SLOTS, E]),
                                             tend[:, :].unsqueeze(1).broadcast_to([1, SLOTS, E]), ALU.is_ge))
                steps.then(dve.tensor_reduce(eidf[:, :], c2, AX_X, ALU.add))
                steps.then(dve.tensor_tensor(c2, c2, ntile[:, :].unsqueeze(1).broadcast_to([1, SLOTS, E]), ALU.mult))
                steps.then(dve.tensor_reduce(offf[:, :], c2, AX_X, ALU.add))
                steps.then(dve.tensor_tensor(offf[:, :], sidx[:, :], offf[:, :], ALU.subtract))
                steps.then(dve.tensor_scalar(offf[:, :], offf[:, :], float(P), None, ALU.mult))
                steps.then(dve.scalar_tensor_tensor(roff[:, :], eidf[:, :], float(REGION), offf[:, :], ALU.mult, ALU.add))
                dve.tensor_scalar(row_of[:, :], roff[:, :], float(E * REGION), None, ALU.min)
                dve.tensor_scalar(weights_at[:, :], eidf[:, :], float(E - 1), float(F), ALU.min, ALU.mult)
                steps.then(dve.tensor_scalar(biases_at[:, :], eidf[:, :], float(E - 1), float(BIAS), ALU.min, ALU.mult))
                dve.tensor_copy(carry[:, :], base[:, :]).then_inc(table_ready, 1)

            def experts(p):
                def later(s, n):
                    return p > 0 or not isinstance(s, int) or s >= n

                def x_rest(s, u):
                    g, k = SLOTS * p + s, u % 2
                    dve.wait_ge(xh_ready, g + 1)
                    dve.tensor_tensor(xl[:, k * P:(k + 1) * P], bank(k, 0, P), xh[:, k * P:(k + 1) * P].bitcast(F32),
                                      ALU.subtract).then_inc(xl_ready, 1)

                def relu(s, u):
                    g, k = SLOTS * p + s, u % 2
                    dve.wait_ge(hT_ps, g + 1)
                    if later(s, 2):
                        dve.wait_ge(y_ps, g - 1)
                    for c in range(FC):
                        ins = dve.tensor_scalar(hT[:, k * F + c * P:k * F + (c + 1) * P], bank(4 + k, c * P, (c + 1) * P),
                                                biases[:, c:][:, bass.ds(b_at[u], 1)], 0.0, ALU.add, ALU.max)
                    ins.then_inc(hT_sb, 1)

                def add_b2(s, u):
                    g, k, r = SLOTS * p + s, u % 2, u % RING
                    lap = s // RING if isinstance(s, int) else s_lap[0] + u // RING
                    dve.wait_ge(y_ps, g + 1)
                    if later(s, RING):
                        dve.wait_ge(y_sent[r], 16 * (LAPS * p + lap))
                    dve.tensor_tensor(ys[:, r * D:(r + 1) * D], bank(6 + k, 0, D), biases[:, FC:][:, bass.ds(b_at[u], D)], ALU.add).then_inc(y_sb, 1)

                def step(s, u):
                    known = isinstance(s, int)
                    if not known or s + 2 < SLOTS:
                        x_rest(s + 2, u + 2)
                    if not known or 0 <= s < SLOTS:
                        relu(s, u)
                    if not known or s >= 1:
                        add_b2(s - 1, u - 1)

                s_lap, b_at = [0], {}
                b_at.update(expert_offsets(DVE, biases_at, BIAS, 0, 0, RING + 4))
                for s in range(-2, RING + 3):
                    step(s, s)
                with dve.Fori(1, LAPS - 1) as lap:
                    s_lap[0] = lap
                    b_at.update(expert_offsets(DVE, biases_at, BIAS, 0, lap * RING, RING + 4))
                    for u in range(3, RING + 3):
                        step(lap * RING + u, u)
                tail = (LAPS - 1) * RING
                b_at.update(expert_offsets(DVE, biases_at, BIAS, tail, tail, RING))
                for s in range(tail + 3, SLOTS + 1):
                    step(s, s)

            def sum_results(b, tiles, z, r):
                def w(j, k):
                    c = (b * TB + j) * 2 + k
                    return wts[:, c:c + 1]

                for j in tiles:
                    c = (b * TB + j) * D
                    ins = dve.scalar_tensor_tensor(r[:, j * D:(j + 1) * D], z[:, 2 * j * D:(2 * j + 1) * D], w(j, 0), tgt[:, c:c + D], ALU.mult, ALU.add)
                steps.then(ins)
                for j in tiles:
                    rj = r[:, j * D:(j + 1) * D]
                    ins = dve.scalar_tensor_tensor(rj, z[:, (2 * j + 1) * D:(2 * j + 2) * D], w(j, 1), rj, ALU.mult, ALU.add)
                return ins

            def merge_tiles(b, tiles):
                h = tiles[0] * 2 // TB
                dve.wait_ge(z_loaded[h], 16 * (b + 1))
                sum_results(b, tiles, zb, sum_r).then_inc(z_used, 1)
                dve.wait_ge(z_used, 2 * b + h + 1)
                return tile_stats(st_r, sum_tile, tiles)

            def center(n, r):
                dve.wait_ge(ln_stats, n + 1)
                for j in range(TB):
                    rj = r[:, j * D:(j + 1) * D]
                    ins = dve.scalar_tensor_tensor(rj, rj, mv[n % LN][:, j, 0:1], gammab[:, :], ALU.subtract, ALU.mult)
                steps.then(ins)

            def add_centered(b, n, r):
                dve.wait_ge(ln_rstd, n + 1)
                for j in range(TB):
                    xj = x_tile(b)(j)
                    ins = dve.scalar_tensor_tensor(xj, r[:, j * D:(j + 1) * D], rs[n % LN][:, j:j + 1], xj, ALU.mult, ALU.add)
                return ins

            def last_sums(b, n):
                if b == 0:
                    for h in range(2):
                        dve.wait_ge(z_loaded[h], 16 * (BATCHES + 1))
                        steps.then(sum_results(b, range(h * TB // 2, (h + 1) * TB // 2), zs[b], sums[b]))
                else:
                    dve.wait_ge(token_added, b)
                    for j in range(TB):
                        rj, c = sums[b][:, j * D:(j + 1) * D], (b * TB + j) * 2 + 1
                        ins = dve.scalar_tensor_tensor(rj, zs[b][:, (2 * j + 1) * D:(2 * j + 2) * D], wts[:, c:c + 1], rj, ALU.mult, ALU.add)
                    steps.then(ins)
                dve.wait_ge(ln_stats, n)
                linked(tile_stats(st_r, lambda j: sums[b][:, j * D:(j + 1) * D]))
                batch_stats(st_r, n)

            def last_add(b):
                dve.wait_ge(gained, b + 1)
                dve.wait_ge(beta_added, BATCHES + b + 1)
                xb = x[:, b * TB * D:(b + 1) * TB * D]
                dve.tensor_tensor(xb, xb, sums[b][:, :], ALU.add).then_inc(x_done, 1)

            def xnT_rest(b):
                dve.wait_ge(xnTh_sb, b + 1)
                dve.tensor_tensor(xnTl[:, :], banks[:, 4 * 512:6 * 512], xnTh[:, :].bitcast(F32), ALU.subtract).then_inc(xnTl_sb, 1)

            def xm_rest(b):
                for m in range(4):
                    h = slice(m * 512, (m + 1) * 512)
                    dve.wait_ge(xmh_sb, 4 * b + m + 1)
                    dve.tensor_tensor(xml[:, h], bank(m), xmh[:, h].bitcast(F32), ALU.subtract).then_inc(xml_sb, 1)

            def add_values(b, g):
                dve.wait_ge(so_ready, GROUPS * b + g + 1)
                for q in range(QG):
                    i = g * QG + q
                    xi = x_tile(b)(i)
                    ins = dve.scalar_tensor_tensor(xi, bank(6, q * P, (q + 1) * P), so[:, i:i + 1], xi, ALU.mult, ALU.add)
                ins.then_inc(values_added, 1)
                dve.wait_ge(values_added, GROUPS * b + g + 1)

            def attention(b, n):
                def maxima(i):
                    for m in range(2):
                        c = slice(2 * i + m, 2 * i + m + 1)
                        dve.wait_ge(s_ps, 2 * (TB * b + i) + m + 1)
                        steps.then(dve.tensor_reduce(mx[:, c], banks[:, 2 * m * 512:(2 * m + 2) * 512], AX_X, ALU.max))
                        dve.tensor_scalar(nb[:, c], mx[:, c], -SCALE, None, ALU.mult).then_inc(nb_ready, 1)

                def difference(i):
                    c = slice(i, i + 1)
                    dve.wait_ge(p_ready, 2 * (TB * b + i) + 2)
                    dve.reciprocal(r1[:, c], l1[:, c])
                    steps.then(dve.reciprocal(r2[:, c], l2[:, c]))
                    steps.then(dve.tensor_scalar(cc[:, c], l1[:, c], r2[:, c], nlam[:, 0:1], ALU.mult, ALU.mult))
                    pp = p1[(TB * b + i) % 3]
                    dve.scalar_tensor_tensor(pp, p2[i % 2], cc[:, c], pp, ALU.mult, ALU.add).then_inc(diff_ready, 1)

                last, after = b > 0, b < BATCHES - 1
                a = BATCHES + b - 1
                for i in range(TB):
                    maxima(i)
                    if i:
                        difference(i - 1)
                    if after and i == 0:
                        merge_tiles(b + 1, range(TB // 2))
                    if after and i == 1:
                        linked(merge_tiles(b + 1, range(TB // 2, TB)))
                        batch_stats(st_r, n)
                        n += 1
                    if last and i == 4:
                        add_values(b - 1, 1)
                        x_stats(b - 1, n)
                        n += 1
                    if after and i == 5:
                        dve.wait_ge(merged, b + 1)
                        x_stats(b + 1, n)
                        n += 1
                difference(TB - 1)
                if last:
                    read_logits(a)
                if after:
                    xnT_rest(b + 1)
                if last:
                    choose(a)
                if after:
                    xm_rest(b + 1)
                add_values(b, 0)
                if last:
                    place(a, b - 1)
                return n

            for b in range(2):
                dve.wait_ge(x_loaded[b], 16)
                x_stats(b, b)
            router_weights()
            for b in range(2, BATCHES):
                dve.wait_ge(x_loaded[b], 16)
                x_stats(b, b)
            for b in range(BATCHES):
                route(0, b)
                if b == 0:
                    small_weights()
                if 0 < b < 3:
                    weights(range((b - 1) * E // 2, b * E // 2))
            minus_lambda()
            dve.wait_ge(qkT_ps, 1)
            dve.tensor_copy(qkwT[:, :], bank(4)).then_inc(qkT_sb, 1)
            dve.wait_ge(M_ps, 1)
            steps.then(dve.tensor_copy(Mh[:, :], bank(3, 0, 2 * D)))
            dve.tensor_tensor(Ml[:, :], bank(3, 0, 2 * D), Mh[:, :].bitcast(F32), ALU.subtract).then_inc(M_sb, 1)
            table()
            experts(0)
            n = BATCHES
            for h in range(2):
                ins = merge_tiles(0, range(h * TB // 2, (h + 1) * TB // 2))
            linked(ins)
            batch_stats(st_r, n)
            center(n, sum_r)
            dve.wait_ge(beta_added, 1)
            steps.then(add_centered(0, n, sum_r))
            x_stats(0, n + 1)
            xnT_rest(0)
            xm_rest(0)
            n += 2
            for b in range(BATCHES):
                n = attention(b, n)
            add_values(BATCHES - 1, 1)
            x_stats(BATCHES - 1, n)
            route(1, BATCHES - 1)
            table()
            experts(1)
            for b in range(BATCHES):
                last_sums(b, n + 1 + b)
                if b >= 2:
                    last_add(b - 2)
            center(n + BATCHES, sums[BATCHES - 1])
            last_add(BATCHES - 2)
            dve.wait_ge(beta_added, 2 * BATCHES)
            add_centered(BATCHES - 1, n + BATCHES, sums[BATCHES - 1]).then_inc(x_done, 1)


_INS = ['L0_attn_x', 'L0_attn_w_q12', 'L0_attn_w_k12', 'L0_attn_w_v', 'L0_attn_lambda_q1', 'L0_attn_lambda_k1',
        'L0_attn_lambda_q2', 'L0_attn_lambda_k2', 'L0_ffn_Wr', 'L0_ffn_br', 'L0_ffn_W1', 'L0_ffn_b1', 'L0_ffn_W2',
        'L0_ffn_b2', 'L0_ffn_gamma', 'L0_ffn_beta']
_OUTS = [((4, 1024, 128), 'float32')]


def kernel(**inputs):
    import numpy as _np
    import concourse.bacc as _bacc
    from concourse import mybir as _mybir
    from concourse.bass_utils import run_bass_kernel_spmd as _run

    nc = _bacc.Bacc("TRN2", target_bir_lowering=False, num_devices=1)
    arrays, args = {}, []
    for name in _INS:
        a = _np.ascontiguousarray(inputs[name])
        arrays[f"in_{name}_dram"] = a
        args.append(nc.dram_tensor(f"in_{name}_dram", a.shape, _mybir.dt.from_np(a.dtype), kind="ExternalInput").ap())
    for i, (shape, dtype) in enumerate(_OUTS):
        dt = _mybir.dt.from_np(_np.dtype(dtype))
        args.append(nc.dram_tensor(f"out_{i}_dram", shape, dt, kind="ExternalOutput").ap())
    macaron_kernel(nc, *args)
    r = _run(nc, [arrays], core_ids=[0])
    return r.results[0]["out_0_dram"]
```
